# Optimizing a Trainium2 kernel written in Bass

```python
import numpy as np
import jax
import jax.numpy as jnp

def _softmax(x, axis=-1):
    return jax.nn.softmax(x, axis=axis)

def _gelu(x):
    return jax.nn.gelu(x, approximate=True)

def _silu(x):
    return jax.nn.silu(x)

def _sigmoid(x):
    return jax.nn.sigmoid(x)

def _layernorm(x, axis=-1, eps=1e-05):
    m = jnp.mean(x, axis=axis, keepdims=True)
    v = jnp.var(x, axis=axis, keepdims=True)
    return (x - m) / jnp.sqrt(v + eps)

def _scatter_add(tgt, idx, src, axis=0):
    return tgt.at[idx].add(src)

def _segment_sum(src, seg, n):
    return jax.ops.segment_sum(src, seg, n)
kernel_name = 'mk_flamingo_gated_d2_seqx_r8_4b49d9'

def setup_inputs(seed: int=0):
    np.random.seed(seed)
    _w = jnp.asarray

    def _rec_inputs():
        import jax
        import jax.numpy as jnp
        _rk = jax.random.key(seed)
        x = -0.0002928 + 1 * jax.random.normal(jax.random.fold_in(_rk, 1), (8, 128, 128), jnp.float32)
        _lenS = 128 - jax.random.randint(jax.random.fold_in(_rk, 7), (8,), 0, max(1, 128 // 4) + 1, jnp.int32)
        _lenS2 = 128 - jax.random.randint(jax.random.fold_in(_rk, 8), (8,), 0, max(1, 128 // 4) + 1, jnp.int32)
        _ctx_1024P = jax.random.normal(jax.random.fold_in(_rk, 11), (8, 16, 128), jnp.float32)
        _ctx_1024c = jax.random.dirichlet(jax.random.fold_in(_rk, 511), 0.3 * jnp.ones((16,), jnp.float32), (8, 128))
        _ctx_1024t = jnp.einsum('bsk,bkd->bsd', _ctx_1024c, _ctx_1024P)
        _ctx_1024t = _ctx_1024t * jax.lax.rsqrt(jnp.mean(jnp.square(_ctx_1024t)) + 1e-12) * 0.953939
        ctx_1024 = 4.13588e-05 + 0.999923 * (_ctx_1024t + 0.3 * jax.random.normal(jax.random.fold_in(_rk, 611), (8, 128, 128), jnp.float32))
        _g = jax.random.normal(jax.random.fold_in(_rk, 9001), (2, 2), jnp.float32)
        _g = jnp.sign(_g) * jnp.maximum(jnp.abs(_g), 1.0) + (_g == 0) * 1.0
        g_xattn = _g[0]
        g_ffn = _g[1]
        return (x, ctx_1024, g_xattn, g_ffn)
    x, ctx_1024, g_xattn, g_ffn = _rec_inputs()

    def _L0_xattn_setup():
        import jax, jax.numpy as jnp
        import numpy as np
        FEATURE_DIM = 128
        NUM_HEADS = 16
        HEAD_DIM = FEATURE_DIM // NUM_HEADS
        key = jax.random.key(seed)
        ks = jax.random.split(key, 11)
        B, SQ, SKV, D = (4, 128, 256, FEATURE_DIM)
        s = 1.0 / np.sqrt(D)
        return {'query': jax.random.normal(ks[0], (B, SQ, D), jnp.float32), 'key': jax.random.normal(ks[1], (B, SKV, D), jnp.float32), 'value': jax.random.normal(ks[2], (B, SKV, D), jnp.float32), 'wq': jax.random.normal(ks[3], (D, D), jnp.float32) * s, 'bq': jnp.zeros((D,), jnp.float32), 'wk': jax.random.normal(ks[4], (D, D), jnp.float32) * s, 'bk': jnp.zeros((D,), jnp.float32), 'wv': jax.random.normal(ks[5], (D, D), jnp.float32) * s, 'bv': jnp.zeros((D,), jnp.float32), 'wo': jax.random.normal(ks[6], (D, D), jnp.float32) * s, 'bo': jnp.zeros((D,), jnp.float32)}
    _L0_xattn_all = _L0_xattn_setup()
    _L0_xattn_in = {k: v for k, v in _L0_xattn_all.items() if k in ('wq', 'bq', 'wk', 'bk', 'wv', 'bv', 'wo', 'bo')}
    del _L0_xattn_all

    def _L0_ffn_setup():
        import jax, jax.numpy as jnp
        import numpy as np
        TOPK = 4
        N_GROUPS = 4
        TOPK_GROUPS = 2
        ROUTE_SCALE = 2.5

        def _gate(x2, Wg):
            T = x2.shape[0]
            E = Wg.shape[0]
            scores = x2 @ Wg.T
            s = jax.nn.sigmoid(scores)
            g = s.reshape(T, N_GROUPS, E // N_GROUPS)
            group_scores = g.max(axis=-1)
            _, gidx = jax.lax.top_k(group_scores, TOPK_GROUPS)
            group_mask = jnp.any(jax.nn.one_hot(gidx, N_GROUPS, dtype=jnp.bool_), axis=1)
            masked = jnp.where(group_mask[:, :, None], g, -jnp.inf).reshape(T, E)
            _, idx = jax.lax.top_k(masked, TOPK)
            w = jnp.take_along_axis(s, idx, axis=1)
            w = w / jnp.sum(w, axis=-1, keepdims=True)
            w = w * ROUTE_SCALE
            return (w.astype(x2.dtype), idx)
        key = jax.random.key(seed)
        ks = jax.random.split(key, 6)
        B, S, D, I, E = (2, 256, 128, 128, 16)
        scale = 0.02
        return {'x': jax.random.normal(ks[0], (B, S, D), dtype=jnp.float32), 'Wg': jax.random.normal(ks[1], (E, D), dtype=jnp.float32) * scale, 'W1': jax.random.normal(ks[2], (E, I, D), dtype=jnp.float32) * scale, 'b1': jnp.zeros((E, I), dtype=jnp.float32), 'W2': jax.random.normal(ks[3], (E, D, I), dtype=jnp.float32) * scale, 'b2': jnp.zeros((E, D), dtype=jnp.float32), 'W3': jax.random.normal(ks[4], (E, I, D), dtype=jnp.float32) * scale, 'b3': jnp.zeros((E, I), dtype=jnp.float32)}
    _L0_ffn_all = _L0_ffn_setup()
    _L0_ffn_in = {k: v for k, v in _L0_ffn_all.items() if k in ('Wg', 'W1', 'b1', 'W2', 'b2', 'W3', 'b3')}
    del _L0_ffn_all

    def _L1_xattn_setup():
        import jax, jax.numpy as jnp
        import numpy as np
        EMBED = 128
        B, I, J = (8, 256, 256)
        SCALE = EMBED ** (-0.5)
        key = jax.random.key(seed)
        ks = jax.random.split(key, 5)
        s = EMBED ** (-0.5)
        return {'q_in': jax.random.normal(ks[0], (B, I, EMBED), dtype=jnp.float32), 'k_v': jax.random.normal(ks[1], (B, J, EMBED), dtype=jnp.float32), 'Wq': jax.random.normal(ks[2], (EMBED, EMBED), dtype=jnp.float32) * s, 'bq': jnp.zeros((EMBED,), dtype=jnp.float32), 'Wk': jax.random.normal(ks[3], (EMBED, EMBED), dtype=jnp.float32) * s, 'bk': jnp.zeros((EMBED,), dtype=jnp.float32), 'Wv': jax.random.normal(ks[4], (EMBED, EMBED), dtype=jnp.float32) * s, 'bv': jnp.zeros((EMBED,), dtype=jnp.float32)}
    _L1_xattn_all = _L1_xattn_setup()
    _L1_xattn_in = {k: v for k, v in _L1_xattn_all.items() if k in ('Wq', 'bq', 'Wk', 'bk', 'Wv', 'bv')}
    del _L1_xattn_all

    def _L1_ffn_setup():
        import jax, jax.numpy as jnp
        import numpy as np
        D_MODEL = 128
        key = jax.random.key(seed)
        k_x, k_w, k_a1, k_a2 = jax.random.split(key, 4)
        x = jax.random.normal(k_x, (4, 256, D_MODEL), dtype=jnp.float32)
        weight = jax.random.normal(k_w, (D_MODEL, D_MODEL), dtype=jnp.float32) * 0.02
        aux_weight1 = jax.random.normal(k_a1, (D_MODEL, D_MODEL), dtype=jnp.float32) * 0.02
        aux_weight2 = jax.random.normal(k_a2, (D_MODEL, D_MODEL), dtype=jnp.float32) * 0.02
        bias = jnp.zeros((D_MODEL,), dtype=jnp.float32)
        return {'x': x, 'weight': weight, 'aux_weight1': aux_weight1, 'aux_weight2': aux_weight2, 'bias': bias}
    _L1_ffn_all = _L1_ffn_setup()
    _L1_ffn_in = {k: v for k, v in _L1_ffn_all.items() if k in ('weight', 'aux_weight1', 'aux_weight2', 'bias')}
    del _L1_ffn_all
    return {'x': x, 'ctx_1024': ctx_1024, 'g_xattn': g_xattn, 'g_ffn': g_ffn, 'L0_xattn_wq': _L0_xattn_in['wq'], 'L0_xattn_bq': _L0_xattn_in['bq'], 'L0_xattn_wk': _L0_xattn_in['wk'], 'L0_xattn_bk': _L0_xattn_in['bk'], 'L0_xattn_wv': _L0_xattn_in['wv'], 'L0_xattn_bv': _L0_xattn_in['bv'], 'L0_xattn_wo': _L0_xattn_in['wo'], 'L0_xattn_bo': _L0_xattn_in['bo'], 'L0_ffn_Wg': _L0_ffn_in['Wg'], 'L0_ffn_W1': _L0_ffn_in['W1'], 'L0_ffn_b1': _L0_ffn_in['b1'], 'L0_ffn_W2': _L0_ffn_in['W2'], 'L0_ffn_b2': _L0_ffn_in['b2'], 'L0_ffn_W3': _L0_ffn_in['W3'], 'L0_ffn_b3': _L0_ffn_in['b3'], 'L1_xattn_Wq': _L1_xattn_in['Wq'], 'L1_xattn_bq': _L1_xattn_in['bq'], 'L1_xattn_Wk': _L1_xattn_in['Wk'], 'L1_xattn_bk': _L1_xattn_in['bk'], 'L1_xattn_Wv': _L1_xattn_in['Wv'], 'L1_xattn_bv': _L1_xattn_in['bv'], 'L1_ffn_weight': _L1_ffn_in['weight'], 'L1_ffn_aux_weight1': _L1_ffn_in['aux_weight1'], 'L1_ffn_aux_weight2': _L1_ffn_in['aux_weight2'], 'L1_ffn_bias': _L1_ffn_in['bias']}

def reference(x, ctx_1024, g_xattn, g_ffn, L0_xattn_wq, L0_xattn_bq, L0_xattn_wk, L0_xattn_bk, L0_xattn_wv, L0_xattn_bv, L0_xattn_wo, L0_xattn_bo, L0_ffn_Wg, L0_ffn_W1, L0_ffn_b1, L0_ffn_W2, L0_ffn_b2, L0_ffn_W3, L0_ffn_b3, L1_xattn_Wq, L1_xattn_bq, L1_xattn_Wk, L1_xattn_bk, L1_xattn_Wv, L1_xattn_bv, L1_ffn_weight, L1_ffn_aux_weight1, L1_ffn_aux_weight2, L1_ffn_bias):
    import jax
    import jax.numpy as jnp

    def _L0_xattn_ref(query, key, value, wq, bq, wk, bk, wv, bv, wo, bo):
        import jax, jax.numpy as jnp
        import numpy as np
        FEATURE_DIM = 128
        NUM_HEADS = 16
        HEAD_DIM = FEATURE_DIM // NUM_HEADS
        B, SQ, D = query.shape
        H, HD = (NUM_HEADS, HEAD_DIM)
        q = (query @ wq.T + bq).reshape(B, SQ, H, HD).transpose(0, 2, 1, 3)
        k = (key @ wk.T + bk).reshape(B, -1, H, HD).transpose(0, 2, 1, 3)
        v = (value @ wv.T + bv).reshape(B, -1, H, HD).transpose(0, 2, 1, 3)
        scores = jnp.einsum('bhqd,bhkd->bhqk', q, k) / jnp.sqrt(jnp.asarray(HD, q.dtype))
        attn = jax.nn.softmax(scores, axis=-1)
        ctx = jnp.einsum('bhqk,bhkd->bhqd', attn, v)
        ctx = ctx.transpose(0, 2, 1, 3).reshape(B, SQ, D)
        return ctx @ wo.T + bo

    def _L0_ffn_ref(x, Wg, W1, b1, W2, b2, W3, b3):
        import jax, jax.numpy as jnp
        import numpy as np
        TOPK = 4
        N_GROUPS = 4
        TOPK_GROUPS = 2
        ROUTE_SCALE = 2.5

        def _gate(x2, Wg):
            T = x2.shape[0]
            E = Wg.shape[0]
            scores = x2 @ Wg.T
            s = jax.nn.sigmoid(scores)
            g = s.reshape(T, N_GROUPS, E // N_GROUPS)
            group_scores = g.max(axis=-1)
            _, gidx = jax.lax.top_k(group_scores, TOPK_GROUPS)
            group_mask = jnp.any(jax.nn.one_hot(gidx, N_GROUPS, dtype=jnp.bool_), axis=1)
            masked = jnp.where(group_mask[:, :, None], g, -jnp.inf).reshape(T, E)
            _, idx = jax.lax.top_k(masked, TOPK)
            w = jnp.take_along_axis(s, idx, axis=1)
            w = w / jnp.sum(w, axis=-1, keepdims=True)
            w = w * ROUTE_SCALE
            return (w.astype(x2.dtype), idx)
        shape = x.shape
        D = shape[-1]
        x2 = x.reshape(-1, D)
        weights, indices = _gate(x2, Wg)
        E = Wg.shape[0]
        y = jnp.zeros_like(x2)
        for e in range(E):
            we = jnp.sum(weights * (indices == e), axis=-1)
            h = jax.nn.silu(x2 @ W1[e].T + b1[e]) * (x2 @ W3[e].T + b3[e])
            y = y + (h @ W2[e].T + b2[e]) * we[:, None]
        return y.reshape(shape)

    def _L1_xattn_ref(q_in, k_v, Wq, bq, Wk, bk, Wv, bv):
        import jax, jax.numpy as jnp
        import numpy as np
        EMBED = 128
        B, I, J = (8, 256, 256)
        SCALE = EMBED ** (-0.5)
        q = q_in @ Wq + bq
        k = k_v @ Wk + bk
        v = k_v @ Wv + bv
        sim = jnp.einsum('bid,bjd->bij', q, k) * SCALE
        attn = jax.nn.softmax(sim, axis=-1)
        out = jnp.einsum('bij,bjd->bid', attn, v)
        return out

    def _L1_ffn_ref(x, weight, aux_weight1, aux_weight2, bias):
        import jax, jax.numpy as jnp
        import numpy as np
        D_MODEL = 128
        h = jnp.einsum('btc,cd->btd', x, weight)
        h = jnp.einsum('btc,cd->btd', h, aux_weight1)
        h = jnp.einsum('btc,cd->btd', h, aux_weight2)
        return jnp.tanh(h + bias)
    x = x + jnp.tanh(g_xattn[0]) * _L0_xattn_ref(_layernorm(x, axis=-1), ctx_1024, ctx_1024, L0_xattn_wq, L0_xattn_bq, L0_xattn_wk, L0_xattn_bk, L0_xattn_wv, L0_xattn_bv, L0_xattn_wo, L0_xattn_bo)
    x = x + jnp.tanh(g_ffn[0]) * _L0_ffn_ref(_layernorm(x, axis=-1), L0_ffn_Wg, L0_ffn_W1, L0_ffn_b1, L0_ffn_W2, L0_ffn_b2, L0_ffn_W3, L0_ffn_b3)
    x = x + jnp.tanh(g_xattn[1]) * _L1_xattn_ref(_layernorm(x, axis=-1), ctx_1024, L1_xattn_Wq, L1_xattn_bq, L1_xattn_Wk, L1_xattn_bk, L1_xattn_Wv, L1_xattn_bv)
    x = x + jnp.tanh(g_ffn[1]) * _L1_ffn_ref(_layernorm(x, axis=-1), L1_ffn_weight, L1_ffn_aux_weight1, L1_ffn_aux_weight2, L1_ffn_bias)
    return x

_drawn_inputs = setup_inputs


def setup_inputs(seed=0):
    import zlib

    import numpy as np

    out = dict(_drawn_inputs(seed))
    spreads = {'g_ffn': (-1.0, 0.6),
     'L0_xattn_bq': (0.0, 0.406),
     'L0_xattn_bk': (0.0, 2.0),
     'L0_xattn_bv': (0.0, 0.1),
     'L0_xattn_bo': (0.0, 0.1),
     'L0_ffn_b1': (0.0, 0.8),
     'L0_ffn_b2': (0.0, 0.387),
     'L0_ffn_b3': (0.0, 0.8),
     'L1_xattn_bq': (0.0, 1.844),
     'L1_xattn_bk': (0.0, 2.0),
     'L1_xattn_bv': (0.0, 0.404),
     'L1_ffn_bias': (0.0, 0.8)}
    factors = {'L0_ffn_W1': 8.0,
     'L0_ffn_W2': 8.0,
     'L0_ffn_W3': 8.0,
     'L1_ffn_weight': 7.528,
     'L1_ffn_aux_weight1': 7.318,
     'L1_ffn_aux_weight2': 7.412}
    for name, (base, spread) in spreads.items():
        noise = np.random.default_rng([zlib.crc32(name.encode()), seed]).standard_normal(out[name].shape)
        drawn = base * np.exp(spread * noise) if base else spread * noise
        out[name] = jnp.asarray(drawn.astype(out[name].dtype))
    for name, factor in factors.items():
        out[name] = (out[name] * factor).astype(out[name].dtype)
    return out
```

```python
import numpy as np

import concourse.bass as bass
from concourse import mybir
from contextlib import ExitStack

F32 = mybir.dt.float32
F32R = mybir.dt.float32r
BF16 = mybir.dt.bfloat16
F16 = mybir.dt.float16
U32 = mybir.dt.uint32
ALU = mybir.AluOpType
ACT = mybir.ActivationFunctionType
AX = mybir.AxisListType.X

P = 128
D = 128
B = 8
HALVES = 2
HB = B // HALVES
HT = HB * P
T = B * P
H = 16
HD = D // H
E = 16
G = 4
EG = E // G
EPS = 1e-5
ROUTE_SCALE = 2.5
BIG = 3.0e38
TAKEN = 3.3e38

A_WK, A_WQ, A_ID, A_COL = 0, D, 2 * D, 3 * D
A_W = 3 * D + 4
(W_V, W_O, W_Q1, W_K1, W_F, W_A1, W_A2, W_G, W_LOW) = (0, 256, 384, 512, 640, 768, 896, 1024, 1024 + E)
B_W = W_LOW + G * G

Q_PARTS = (0, 0, 0, 1, 1, 2)
K_PARTS = (0, 1, 2, 0, 1, 0)
MAX_ROW = HD * len(Q_PARTS)

GROUPS = 4
GH = H // GROUPS
NG = B * GROUPS
ST_LAG = 9
AV_LAG = ST_LAG + 3
VC = 3 * HD + 1
RING = 4


def flamingo(nc, x, ctx_t, w_a, w_b, rows, gates, b2, w_big, b_cols, out):
    scale0 = float(HD) ** -0.5
    scale1 = float(D) ** -0.5
    web_dram = nc.dram_tensor("web_dram", [E, T], F32, kind="Internal").ap()

    stack = ExitStack()
    with stack:
        def sb(name, shape, dt=F32):
            return stack.enter_context(nc.sbuf_tensor(name, shape, dt))

        def sem(name):
            return stack.enter_context(nc.semaphore(name))

        x0 = sb("x0", [P, B, D])
        x1 = sb("x1", [P, B, D])
        x2 = x0
        x3 = x1
        xn = sb("xn", [P, B, D])
        xn_t = sb("xn_t", [P, T])
        xh = sb("xh", [P, T], F32R)
        xl = sb("xl", [P, T], F32R)
        ctx_sb = sb("ctx_sb", [P, T])
        wa = sb("wa", [P, A_W])
        wb = sb("wb", [P, B_W])
        row_sb = sb("row_sb", [P, 4 * D])
        gate_sb = sb("gate_sb", [P, 4])
        tg = sb("tg", [P, 4])
        b2_sb = sb("b2_sb", [E, D])
        b2_twice = sb("b2_twice", [E, D])
        big = sb("big", [P, E, 3 * D])
        bcol = sb("bcol", [P, E, 3])
        stats = sb("stats", [P, B, 6])
        mv = sb("mv", [P, B, 2])
        var_eps = sb("var_eps", [P, B])
        rstd = sb("rstd", [P, B])
        minus_half = sb("minus_half", [P, B])
        identb = sb("identb", [P, P], BF16)
        parts = [sb(f"parts{n}", [P, 3, HT], BF16) for n in range(4)]
        rest = x1[:, :, :].rearrange("p b d -> p (b d)").rearrange("p (s t) -> p s t", s=2)
        qs = sb("qs", [P, H, T], BF16)
        ks = sb("ks", [P, H, T], BF16)
        v_parts = sb("v_parts", [P, B * H, VC], BF16)
        v1 = sb("v1", [P, B, D])
        k1_t = sb("k1_t", [P, T])
        negm = sb("negm", [P, 2, H])
        negm_parts = sb("negm_parts", [P, 2, 2 * H], BF16)
        negm_rows = sb("negm_rows", [2 * H, 2, P], BF16)
        pe = sb("pe", [P, RING, GH * P])
        p1 = sb("p1", [P, RING, GH * P], F16)
        p2 = sb("p2", [P, RING, GH * P], F16)
        o_sum = sb("o_sum", [P, 2, D])
        o_nat = sb("o_nat", [P, 2, D])
        o_t = sb("o_t", [P, 2, P])
        den = sb("den", [P, 2, H])
        wf = sb("wf", [P, 2, D])
        raw = sb("raw", [P, B, E])
        sg = sb("sg", [P, B, E])
        gmax = sb("gmax", [P, B, G])
        cmp_a = sb("cmp_a", [P, B, G, G])
        cmp_b = sb("cmp_b", [P, B, G, G])
        rank = sb("rank", [P, B, G])
        cand = sb("cand", [P, B, 4 + E])
        top8 = sb("top8", [P, B, 8])
        left = sb("left", [P, B, 4 + E])
        wts = sb("wts", [P, B, E])
        wsum = sb("wsum", [P, B])
        wt_t = sb("wt_t", [E, T])
        w13h = sb("w13h", [P, 2, 2 * D], F32R)
        w13l = sb("w13l", [P, 2, 2 * D], F32R)
        w2h = sb("w2h", [P, 2, D], F32R)
        w2l = sb("w2l", [P, 2, D], F32R)
        hh = sb("hh", [P, RING, HT], F32R)
        hl = sb("hl", [P, RING, HT], F32R)
        bslot = sb("bslot", [P, 2, 3])
        qs_free = qs[:, :, :].rearrange("p h t -> p (h t)").bitcast(F32)
        web = qs_free[:, 0:2 * T].rearrange("p (s t) -> p s t", s=2)
        a1 = qs_free[:, 2 * T:3 * T].rearrange("p (s t) -> p s t", s=2)
        th = qs_free[:, 3 * T:4 * T].rearrange("p (s t) -> p s t", s=2)
        uu = qs_free[:, 4 * T:5 * T].rearrange("p (s t) -> p s t", s=2)
        h0 = qs_free[:, 5 * T:6 * T].rearrange("p (s t) -> p s t", s=2)
        hw = qs_free[:, 6 * T:8 * T].rearrange("p (s t) -> p s t", s=RING)
        ks_free = ks[:, :, :].rearrange("p h t -> p (h t)").bitcast(F32)
        y_t = ks_free[:, 0:T]
        q1_t = ks_free[:, T:2 * T]
        pr = ks_free[:, 2 * T:3 * T].rearrange("p (b t) -> p b t", b=B)
        pr_t = ks_free[:, 3 * T:4 * T].rearrange("p (b t) -> p b t", b=B)
        ff = ks_free[:, 4 * T:5 * T].rearrange("p (b t) -> p b t", b=B)
        fft = ks_free[:, 5 * T:6 * T].rearrange("p (b t) -> p b t", b=B)
        x4 = ks_free[:, 6 * T:7 * T].rearrange("p (b t) -> p b t", b=B)
        negm1 = sb("negm1", [P, 2, B])
        den1 = sb("den1", [P, 2, B])

        ps = stack.enter_context(nc.psum_tensor("ps", [P, 8, 512], F32))
        ident = wa[:, A_ID:A_ID + P]

        x_in, ctx_in, wa_in, wb_in, row_in, gate_in, b2_in, big_in, bcol_in = (
            sem(n) for n in ("x_in", "ctx_in", "wa_in", "wb_in", "row_in", "gate_in", "b2_in", "big_in", "bcol_in"))
        rows_in = [sem(f"rows_in{n}") for n in range(4)]
        negm_in = [sem(f"negm_in{n}") for n in range(2)]
        web_in = [sem(f"web_in{n}") for n in range(2)]
        wt_out = sem("wt_out")
        out_done = sem("out_done")
        vec = sem("vec")
        vec_u = sem("vec_u")
        pads, pools_ready = sem("pads"), sem("pools_ready")
        var_ready, rstd_ready, xn_ready, xn_tr, xn_t_ready = (
            sem(n) for n in ("var_ready", "rstd_ready", "xn_ready", "xn_tr", "xn_t_ready"))
        proj_ready, part1, rest_ready, part2, part3 = (
            sem(n) for n in ("proj_ready", "part1", "rest_ready", "part2", "part3"))
        v_proj, v_evac, v_part1, v_rest, v_part2, v_done = (
            sem(n) for n in ("v_proj", "v_evac", "v_part1", "v_rest", "v_part2", "v_done"))
        k1_proj, k1_evac, wf_mm, wf_evac, tg_ready, identb_ready, xb_ready, bcol_ready = (
            sem(n) for n in ("k1_proj", "k1_evac", "wf_mm", "wf_evac", "tg_ready", "identb_ready", "xb_ready",
                             "bcol_ready"))
        s_ready, max_done, negm_ready, t_ready, t_evac = (
            sem(n) for n in ("s_ready", "max_done", "negm_ready", "t_ready", "t_evac"))
        st_ready, exp_done, p1_vec, p2_pool, p2_vec, av_done = (
            sem(n) for n in ("st_ready", "exp_done", "p1_vec", "p2_pool", "p2_vec", "av_done"))
        o_done, o_proj, x1_done = (sem(n) for n in ("o_done", "o_proj", "x1_done"))
        x_split, gate_mm, gate_evac, gate_exp, wts_ready, wts_tr, wt_evac, b2_ready, b2_mm, low_done = (
            sem(n) for n in ("x_split", "gate_mm", "gate_evac", "gate_exp", "wts_ready", "wts_tr", "wt_evac",
                             "b2_ready", "b2_mm", "low_done"))
        a_ready, c_ready, act_t, h0_done, mult_done, hi_done, lo_done, w2_done = (
            sem(n) for n in ("a_ready", "c_ready", "act_t", "h0_done", "mult_done", "hi_done", "lo_done", "w2_done"))
        w13_hi, w13_lo, w2_hi, w2_lo, bias_ready = (
            sem(n) for n in ("w13_hi", "w13_lo", "w2_hi", "w2_lo", "bias_ready"))
        y_evac, y_tr, q1_mm, q1_evac, s1_mm, negm1_done, p_done, p_tr, p_evac, av1_mm, f_mm, f_add, f_tanh, x4_done = (
            sem(n) for n in ("y_evac", "y_tr", "q1_mm", "q1_evac", "s1_mm", "negm1_done", "p_done", "p_tr", "p_evac",
                             "av1_mm", "f_mm", "f_add", "f_tanh", "x4_done"))

        def wait(eng, s, count):
            if not isinstance(count, int) or count > 0:
                eng.wait_ge(s, count)

        def tok(b):
            return slice(b * P, (b + 1) * P)

        def half(h):
            return slice(h * HT, (h + 1) * HT)

        def seqs(h):
            return slice(h * HB, (h + 1) * HB)

        def flat(ap):
            return ap.rearrange("p b t -> p (b t)")

        def by_vec(j):
            return j % GROUPS == GROUPS - 1

        def wait_p2(eng, j):
            if j >= 0:
                if by_vec(j):
                    eng.wait_ge(p2_vec, j // GROUPS + 1)
                else:
                    eng.wait_ge(p2_pool, j - j // GROUPS + 1)

        def t_before_negm(b):
            return b + max(0, b - 3)

        def t_before_o(b):
            return min(B, b + 4) + b

        block = stack.enter_context(nc.Block())

        @block.sync
        def _(sp):
            sp.dma_start(x0[:, :, :], x.rearrange("b t d -> t b d")).then_inc(x_in, 16)
            sp.dma_start(ctx_sb[:, :], ctx_t).then_inc(ctx_in, 16)
            sp.dma_start(wa[:, :], w_a).then_inc(wa_in, 16)
            sp.dma_start(wb[:, :], w_b).then_inc(wb_in, 16)
            sp.dma_start(row_sb[:, :], rows.partition_broadcast(P)).then_inc(row_in, 16)
            sp.dma_start(gate_sb[:, :], gates.partition_broadcast(P)).then_inc(gate_in, 16)
            for n in range(4):
                dst, terms = (qs, Q_PARTS) if n % 2 else (ks, K_PARTS)
                sp.wait_ge(pads, n + 1)
                for part, ready in enumerate((part1, part2, part3)):
                    sp.wait_ge(ready, n + 1)
                    for r, term in enumerate(terms):
                        if term == part:
                            sp.dma_start(dst[r * HD:(r + 1) * HD, :, half(n // 2)],
                                         parts[n][:, part, :]).then_inc(rows_in[n], 16)
            sp.dma_start(b2_sb[:, :], b2).then_inc(b2_in, 16)
            sp.dma_start(bcol[:, :, 1:3], b_cols).then_inc(bcol_in, 16)
            sp.dma_start(big[:, :, :], w_big).then_inc(big_in, 16)
            for b in range(B):
                sp.wait_ge(t_evac, t_before_negm(b) + 1)
                sp.dma_start(qs[MAX_ROW:MAX_ROW + 2, :, tok(b)], negm_rows[:, b % 2, :]).then_inc(negm_in[b % 2], 16)
            sp.wait_ge(wt_evac, HALVES)
            sp.dma_start(web_dram, wt_t[:, :]).then_inc(wt_out, 16)
            sp.wait_ge(wt_out, 16)

            def bring(e, s):
                wait(sp, mult_done, 2 * e - 2)
                sp.dma_start(web[:, s, :], web_dram[bass.ds(e, 1), :].partition_broadcast(P)).then_inc(web_in[s], 16)

            for e in (0, 1):
                sp.dma_start(web[:, e, :], web_dram[e:e + 1, :].partition_broadcast(P)).then_inc(web_in[e], 16)
            with sp.Fori(2, E - 1, 2) as e:
                bring(e, 0)
                bring(e + 1, 1)
            out_t = out.rearrange("b t d -> t b d")
            for h in range(HALVES):
                sp.wait_ge(x4_done, h + 1)
                sp.dma_start(out_t[:, seqs(h), :], x4[:, seqs(h), :]).then_inc(out_done, 16)
            sp.wait_ge(out_done, 16 * HALVES)

        @block.gpsimd
        def _(pool):
            pool.memset(minus_half[:, :], -0.5).then_inc(pools_ready, 1)
            pool.memset(ks[:, :, 0:HT], 1.0).then_inc(pads, 1)
            pool.memset(qs[:, :, 0:HT].bitcast(U32), 0).then_inc(pads, 1)
            pool.wait_ge(pools_ready, 1)
            pool.wait_ge(var_ready, 1)
            pool.tensor_tensor(rstd[:, :], var_eps[:, :], minus_half[:, :], ALU.pow).then_inc(rstd_ready, 1)
            pool.memset(ks[:, :, HT:T], 1.0).then_inc(pads, 1)
            pool.memset(qs[:, :, HT:T].bitcast(U32), 0).then_inc(pads, 1)
            pool.memset(v_parts[:, :, VC - 1:VC], 1.0).then_inc(pools_ready, 1)
            for h in range(HALVES):
                hv = slice(h * HB * H, (h + 1) * HB * H)
                vf = flat(xn[:, seqs(h), :]).rearrange("p (n d) -> p n d", d=HD)
                pool.wait_ge(v_part1, h + 1)
                pool.tensor_tensor(vf, vf, v_parts[:, hv, 2 * HD:3 * HD], ALU.subtract).then_inc(v_rest, 1)
                pool.wait_ge(v_part2, h + 1)
                pool.tensor_tensor(v_parts[:, hv, 0:HD], vf, v_parts[:, hv, HD:2 * HD], ALU.subtract).then_inc(v_done, 1)
            for j in range(NG):
                if not by_vec(j):
                    pool.wait_ge(p1_vec, j - j // GROUPS + 1)
                    wait(pool, av_done, j - RING + 1)
                    pool.tensor_tensor(p2[:, j % RING, :], pe[:, j % RING, :], p1[:, j % RING, :],
                                       ALU.subtract).then_inc(p2_pool, 1)
            for h in range(HALVES):
                pool.wait_ge(var_ready, 2 + h)
                pool.tensor_tensor(rstd[:, seqs(h)], var_eps[:, seqs(h)], minus_half[:, seqs(h)],
                                   ALU.pow).then_inc(rstd_ready, 1)

            def split13(e, s):
                pool.wait_ge(w13_hi, e + 1)
                pool.tensor_tensor(w13l[:, s, :], big[:, bass.ds(e, 1), 0:2 * D].rearrange("p e w -> p (e w)"),
                                   w13h[:, s, :].bitcast(F32), ALU.subtract).then_inc(w13_lo, 1)
                wait(pool, h0_done, 2 * e - 2)
                pool.tensor_copy(bslot[:, s, :], bcol[:, bass.ds(e, 1), :].rearrange("p e w -> p (e w)"))\
                    .then_inc(bias_ready, 1)

            def split2(e, s):
                pool.wait_ge(w2_hi, e + 1)
                pool.tensor_tensor(w2l[:, s, :], big[:, bass.ds(e, 1), 2 * D:3 * D].rearrange("p e w -> p (e w)"),
                                   w2h[:, s, :].bitcast(F32), ALU.subtract).then_inc(w2_lo, 1)

            def expert(e, s, n_web, last=False):
                for h in range(HALVES):
                    if h == 0 and not last:
                        split13(e + 1, 1 - s)
                    if h == 1:
                        split2(e, s)
                    if h == 0:
                        pool.wait_ge(web_in[s], n_web)
                    pool.wait_ge(h0_done, 2 * e + h + 1)
                    wait(pool, lo_done, 2 * e + h - RING + 1)
                    pool.tensor_tensor(hw[:, 2 * s + h, :], h0[:, h, :], web[:, s, half(h)],
                                       ALU.mult).then_inc(mult_done, 1)

            pool.wait_ge(bcol_ready, 1)
            split13(0, 0)
            expert(0, 0, 16)
            expert(1, 1, 16)
            with pool.Fori(2, E - 3, 2) as e:
                expert(e, 0, 8 * e + 16)
                expert(e + 1, 1, 8 * e + 16)
            expert(E - 2, 0, 8 * E)
            expert(E - 1, 1, 8 * E, last=True)
            for n in range(2 * HALVES):
                h = n % HALVES
                pool.wait_ge(var_ready, 4 + n)
                pool.tensor_tensor(rstd[:, seqs(h)], var_eps[:, seqs(h)], minus_half[:, seqs(h)],
                                   ALU.pow).then_inc(rstd_ready, 1)

        @block.scalar
        def _(act):
            act.wait_ge(gate_in, 16)
            act.activation(tg[:, :], gate_sb[:, :], ACT.Tanh).then_inc(tg_ready, 1)
            act.wait_ge(wa_in, 16)
            act.activation(identb[:, :], ident, ACT.Copy).then_inc(identb_ready, 1)

            def first_part(n):
                col = A_COL + (1 - n % 2)
                act.wait_ge(proj_ready, n + 1)
                act.activation(parts[n][:, 0, :], ps[:, n, :], ACT.Identity, bias=wa[:, col:col + 1]).then_inc(part1, 1)

            def second_part(n):
                act.wait_ge(rest_ready, n + 1)
                act.activation(parts[n][:, 1, :], rest[:, n % 2, :], ACT.Copy).then_inc(part2, 1)

            for h in range(HALVES):
                first_part(2 * h)
                act.wait_ge(xn_tr, h + 1)
                act.activation(xn_t[:, half(h)], ps[:, 4 + h, :], ACT.Copy).then_inc(xn_t_ready, 1)
                second_part(2 * h)
                first_part(2 * h + 1)
                second_part(2 * h + 1)
            act.wait_ge(pools_ready, 2)
            for h in range(HALVES):
                hv = slice(h * HB * H, (h + 1) * HB * H)
                vf = flat(xn[:, seqs(h), :]).rearrange("p (n d) -> p n d", d=HD)
                act.wait_ge(v_evac, 2 * h + 2)
                act.activation(v_parts[:, hv, 2 * HD:3 * HD], vf, ACT.Copy).then_inc(v_part1, 1)
                act.wait_ge(v_rest, h + 1)
                act.activation(v_parts[:, hv, HD:2 * HD], vf, ACT.Copy).then_inc(v_part2, 1)
            for h in range(HALVES):
                act.wait_ge(k1_proj, h + 1)
                act.activation(k1_t[:, half(h)], ps[:, 4 + h, :], ACT.Identity,
                               bias=wa[:, A_COL + 3:A_COL + 4]).then_inc(k1_evac, 1)
            for n in range(2):
                act.wait_ge(wf_mm, n + 1)
                act.activation(wf[:, n, :], ps[:, 7, 0:D], ACT.Copy).then_inc(wf_evac, 1)
            act.wait_ge(bcol_in, 16)
            act.activation(bcol[:, :, 0:1], bcol[:, :, 1:2], ACT.Copy, scale=0.5).then_inc(bcol_ready, 1)
            act.wait_ge(b2_in, 16)
            act.activation(b2_twice[:, :], b2_sb[:, :], ACT.Copy, scale=2.0).then_inc(b2_ready, 1)

            for step in range(NG + AV_LAG + 6):
                j = step - ST_LAG
                if 0 <= j < NG:
                    act.wait_ge(st_ready, j + 1)
                    wait_p2(act, j - RING)
                    e = act.activation(pe[:, j % RING, :], ps[:, 2 + j % 2, :], ACT.Exp, scale=scale0)
                    if by_vec(j):
                        wait(act, av_done, j - RING + 1)
                        e = act.activation(p1[:, j % RING, :], ps[:, 2 + j % 2, :], ACT.Exp, scale=scale0)
                    e.then_inc(exp_done, 1)
                if step % GROUPS == 1:
                    b = step // GROUPS - 1
                    if 0 <= b < B:
                        act.wait_ge(t_ready, t_before_negm(b) + 1)
                        if b >= 2:
                            act.wait_ge(negm_in[b % 2], 16 * (b // 2))
                        act.activation(negm_rows[:, b % 2, :], ps[0:2 * H, 6, 0:P // 2].bitcast(BF16),
                                       ACT.Copy).then_inc(t_evac, 1)
                    b = step // GROUPS - 4
                    if 0 <= b < B:
                        act.wait_ge(t_ready, t_before_o(b) + 1)
                        wait(act, o_proj, b - 1)
                        act.activation(o_t[:, b % 2, :], ps[:, 6, 0:P], ACT.Copy).then_inc(t_evac, 1)
            for h in range(HALVES):
                act.wait_ge(xn_tr, HALVES + h + 1)
                act.activation(xh[:, half(h)], ps[:, h, :], ACT.Copy).then_inc(x_split, 1)
                act.activation(xn_t[:, half(h)], ps[:, h, :], ACT.Copy).then_inc(xn_t_ready, 1)
            for h in range(HALVES):
                act.wait_ge(gate_evac, h + 1)
                act.activation(sg[:, seqs(h), :], raw[:, seqs(h), :], ACT.Exp, scale=-1.0).then_inc(gate_exp, 1)

            def high13(e, s):
                wait(act, c_ready, 2 * e - 2)
                act.activation(w13h[:, s, :], big[:, bass.ds(e, 1), 0:2 * D].rearrange("p e w -> p (e w)"),
                               ACT.Copy).then_inc(w13_hi, 1)

            def high2(e, s):
                wait(act, w2_done, 2 * e - 2)
                act.activation(w2h[:, s, :], big[:, bass.ds(e, 1), 2 * D:3 * D].rearrange("p e w -> p (e w)"),
                               ACT.Copy).then_inc(w2_hi, 1)

            def high_h(u, slot):
                act.wait_ge(mult_done, u + 1)
                wait(act, w2_done, u - RING + 1)
                act.activation(hh[:, slot, :], hw[:, slot, :], ACT.Copy).then_inc(hi_done, 1)

            def expert(e, s, first=False, last=False):
                for h in range(HALVES):
                    if h == 0:
                        act.wait_ge(bias_ready, e + 1)
                    act.wait_ge(a_ready, 2 * e + h + 1)
                    wait(act, h0_done, 2 * e + h - 1)
                    act.activation(a1[:, h, :], ps[:, h, :], ACT.Identity, bias=bslot[:, s, 1:2])
                    act.activation(th[:, h, :], ps[:, h, :], ACT.Tanh, bias=bslot[:, s, 0:1],
                                   scale=0.5).then_inc(act_t, 1)
                    if h == 0 and not last:
                        high13(e + 1, 1 - s)
                    if h == 1:
                        high2(e, s)
                    if not first:
                        high_h(2 * e + h - 2, 2 * (1 - s) + h)

            act.wait_ge(big_in, 16)
            act.wait_ge(x1_done, B)
            high13(0, 0)
            expert(0, 0, first=True)
            expert(1, 1)
            expert(2, 0)
            expert(3, 1)
            with act.Fori(4, E - 3, 2) as e:
                expert(e, 0)
                expert(e + 1, 1)
            expert(E - 2, 0)
            expert(E - 1, 1, last=True)
            high_h(2 * E - 2, 2)
            high_h(2 * E - 1, 3)

            for h in range(HALVES):
                act.wait_ge(w2_done, 2 * E - 1 + h)
                act.activation(y_t[:, half(h)], ps[:, 6 + h, :], ACT.Copy).then_inc(y_evac, 1)
            for h in range(HALVES):
                act.wait_ge(xn_tr, 2 * HALVES + h + 1)
                act.activation(xn_t[:, half(h)], ps[:, 2 + h, :], ACT.Copy).then_inc(xn_t_ready, 1)
            for h in range(HALVES):
                act.wait_ge(q1_mm, h + 1)
                act.activation(q1_t[:, half(h)], ps[:, 4 + h, :], ACT.Identity,
                               bias=wa[:, A_COL + 2:A_COL + 3]).then_inc(q1_evac, 1)
            for h in range(HALVES):
                act.wait_ge(negm1_done, h + 1)
                for b in range(h * HB, (h + 1) * HB):
                    e = act.activation(pr[:, b, :], ps[:, h, tok(b % HB)], ACT.Exp, scale=scale1,
                                       bias=negm1[:, 1, b:b + 1], accum_out=den1[:, 0, b:b + 1])
                e.then_inc(p_done, 1)
            for h in range(HALVES):
                act.wait_ge(xn_tr, 3 * HALVES + h + 1)
                act.activation(xn_t[:, half(h)], ps[:, h, :], ACT.Copy).then_inc(xn_t_ready, 1)
            for h in range(HALVES):
                act.wait_ge(f_add, h + 1)
                act.activation(fft[:, seqs(h), :], ff[:, seqs(h), :], ACT.Tanh).then_inc(f_tanh, 1)

        @block.tensor
        def _(pe_):
            def transpose_half(h, bank):
                for i in range(HB):
                    t = pe_.transpose(ps[:, bank, tok(i)], xn[:, h * HB + i, :], ident)
                t.then_inc(xn_tr, 1)

            pe_.wait_ge(ctx_in, 16)
            pe_.wait_ge(wa_in, 16)
            for h in range(HALVES):
                pe_.matmul(ps[:, 2 * h, :], wa[:, A_WK:A_WK + D], ctx_sb[:, half(h)], start=True,
                           stop=True).then_inc(proj_ready, 1)
                pe_.wait_ge(xn_ready, h + 1)
                transpose_half(h, 4 + h)
                pe_.wait_ge(xn_t_ready, h + 1)
                pe_.matmul(ps[:, 2 * h + 1, :], wa[:, A_WQ:A_WQ + D], xn_t[:, half(h)], start=True,
                           stop=True).then_inc(proj_ready, 1)
            pe_.wait_ge(wb_in, 16)
            for n in range(4):
                wait(pe_, v_evac, n - 1)
                for i in range(2):
                    m = pe_.matmul(ps[:, 6 + n % 2, i * 2 * D:(i + 1) * 2 * D], ctx_sb[:, tok(2 * n + i)],
                                   wb[:, W_V:W_V + 2 * D], start=True, stop=True)
                m.then_inc(v_proj, 1)
            for h in range(HALVES):
                pe_.matmul(ps[:, 4 + h, :], wb[:, W_K1:W_K1 + D], ctx_sb[:, half(h)], start=True,
                           stop=True).then_inc(k1_proj, 1)
            pe_.wait_ge(v_evac, 4)
            pe_.matmul(ps[:, 7, 0:D], wb[:, W_A1:W_A1 + D], wb[:, W_A2:W_A2 + D], start=True,
                       stop=True).then_inc(wf_mm, 1)
            pe_.wait_ge(wf_evac, 1)
            pe_.matmul(ps[:, 7, 0:D], wb[:, W_F:W_F + D], wf[:, 0, :], start=True, stop=True).then_inc(wf_mm, 1)

            pe_.wait_ge(identb_ready, 1)
            pe_.wait_ge(rest_ready, 4)
            pe_.wait_ge(wf_evac, 2)
            pe_.wait_ge(k1_evac, 2)
            for step in range(NG + AV_LAG + 6):
                j = step
                if j < NG:
                    b, g = divmod(j, GROUPS)
                    if j % (GROUPS * HB) == 0:
                        for n in (0, 1):
                            pe_.wait_ge(rows_in[2 * (b // HB) + n], 16 * len(Q_PARTS))
                    wait(pe_, max_done, j - 1)
                    for i in range(GH):
                        m = pe_.matmul(ps[:, j % 2, tok(i)], qs[:, g * GH + i, tok(b)], ks[:, g * GH + i, tok(b)],
                                       start=True, stop=True)
                    m.then_inc(s_ready, 1)
                j = step - ST_LAG
                if 0 <= j < NG:
                    b, g = divmod(j, GROUPS)
                    if g == 0:
                        pe_.wait_ge(negm_in[b % 2], 16 * (b // 2 + 1))
                    wait(pe_, exp_done, j - 1)
                    for i in range(GH):
                        m = pe_.matmul(ps[:, 2 + j % 2, tok(i)], ks[:, g * GH + i, tok(b)], qs[:, g * GH + i, tok(b)],
                                       start=True, stop=True)
                    m.then_inc(st_ready, 1)
                j = step - AV_LAG
                if 0 <= j < NG:
                    b, g = divmod(j, GROUPS)
                    if j % (GROUPS * HB) == 0:
                        pe_.wait_ge(v_done, b // HB + 1)
                    if g == 0:
                        wait(pe_, o_done, b - 1)
                    wait_p2(pe_, j)
                    for i in range(GH):
                        hd = g * GH + i
                        pe_.matmul(ps[:, 4 + b % 2, hd * VC:(hd + 1) * VC], p1[:, j % RING, tok(i)],
                                   v_parts[:, b * H + hd, :], start=True, stop=True)
                        m = pe_.matmul(ps[:, 4 + b % 2, hd * VC + HD:(hd + 1) * VC], p2[:, j % RING, tok(i)],
                                       v_parts[:, b * H + hd, HD:VC], start=False, stop=True, skip_group_check=True)
                    m.then_inc(av_done, 1)
                if step % GROUPS == 1:
                    b = step // GROUPS - 1
                    if 0 <= b < B:
                        pe_.wait_ge(negm_ready, b + 1)
                        wait(pe_, t_evac, t_before_negm(b))
                        pe_.transpose(ps[0:2 * H, 6, 0:P // 2].bitcast(BF16), negm_parts[:, b % 2, :],
                                      identb[:, :]).then_inc(t_ready, 1)
                    b = step // GROUPS - 4
                    if 0 <= b < B:
                        pe_.wait_ge(o_done, b + 1)
                        wait(pe_, t_evac, t_before_o(b))
                        pe_.transpose(ps[:, 6, 0:P], o_nat[:, b % 2, :], ident).then_inc(t_ready, 1)
                if step % GROUPS == 2:
                    b = step // GROUPS - 4
                    if 0 <= b < B:
                        pe_.wait_ge(t_evac, t_before_o(b) + 1)
                        wait(pe_, x1_done, b)
                        pe_.matmul(ps[:, 7, 0:D], o_t[:, b % 2, :], wb[:, W_O:W_O + D], start=True,
                                   stop=True).then_inc(o_proj, 1)

            for h in range(HALVES):
                pe_.wait_ge(xn_ready, HALVES + h + 1)
                transpose_half(h, h)
            for h in range(HALVES):
                pe_.wait_ge(xn_t_ready, HALVES + h + 1)
                for i in range(HB):
                    m = pe_.matmul(ps[:, 2 + h, i * E:(i + 1) * E], xn_t[:, tok(h * HB + i)], wb[:, W_G:W_G + E],
                                   start=True, stop=True)
                m.then_inc(gate_mm, 1)
            for h in range(HALVES):
                pe_.wait_ge(wts_ready, 1)
                for i in range(HB):
                    t = pe_.transpose(ps[0:E, 4 + h, tok(i)], wts[:, h * HB + i, :], ident)
                t.then_inc(wts_tr, 1)
            pe_.wait_ge(b2_ready, 1)
            for h in range(HALVES):
                pe_.wait_ge(wt_evac, h + 1)
                pe_.matmul(ps[:, 6 + h, :], b2_twice[:, :], wt_t[:, half(h)], start=True, stop=True).then_inc(b2_mm, 1)

            def up(e, s, h):
                if h == 0:
                    pe_.wait_ge(w13_lo, e + 1)
                for bank, col, freed, ready in ((h, 0, act_t, a_ready), (2 + h, D, h0_done, c_ready)):
                    wait(pe_, freed, 2 * e + h - 1)
                    cols = slice(col, col + D)
                    pe_.matmul(ps[:, bank, :], w13h[:, s, cols], xh[:, half(h)], start=True, stop=False)
                    pe_.matmul(ps[:, bank, :], w13h[:, s, cols], xl[:, half(h)], start=False, stop=False)
                    pe_.matmul(ps[:, bank, :], w13l[:, s, cols], xh[:, half(h)], start=False,
                               stop=True).then_inc(ready, 1)

            def down(e, s, h):
                slot = 2 * s + h
                pe_.wait_ge(lo_done, 2 * e + h + 1)
                if h == 0:
                    pe_.wait_ge(w2_lo, e + 1)
                y = ps[:, 6 + h, :]
                pe_.matmul(y, w2h[:, s, :], hh[:, slot, :], start=False, stop=False, skip_group_check=True)
                pe_.matmul(y, w2h[:, s, :], hl[:, slot, :], start=False, stop=False, skip_group_check=True)
                pe_.matmul(y, w2l[:, s, :], hh[:, slot, :], start=False, stop=True,
                           skip_group_check=True).then_inc(w2_done, 1)

            def expert(e, s):
                up(e, s, 0)
                down(e - 2, s, 1)
                up(e, s, 1)
                down(e - 1, 1 - s, 0)

            pe_.wait_ge(low_done, HALVES)
            pe_.wait_ge(gate_evac, HALVES)
            up(0, 0, 0)
            up(0, 0, 1)
            up(1, 1, 0)
            up(1, 1, 1)
            down(0, 0, 0)
            with pe_.Fori(2, E - 1, 2) as e:
                expert(e, 0)
                expert(e + 1, 1)
            down(E - 2, 0, 1)
            down(E - 1, 1, 0)
            down(E - 1, 1, 1)

            for h in range(HALVES):
                pe_.wait_ge(y_evac, h + 1)
                for i in range(HB):
                    t = pe_.transpose(ps[:, h, tok(i)], y_t[:, tok(h * HB + i)], ident)
                t.then_inc(y_tr, 1)
            for h in range(HALVES):
                pe_.wait_ge(xn_ready, 2 * HALVES + h + 1)
                transpose_half(h, 2 + h)
            for h in range(HALVES):
                pe_.wait_ge(xn_t_ready, 2 * HALVES + h + 1)
                pe_.matmul(ps[:, 4 + h, :], wb[:, W_Q1:W_Q1 + D], xn_t[:, half(h)], start=True,
                           stop=True).then_inc(q1_mm, 1)
            for h in range(HALVES):
                pe_.wait_ge(q1_evac, h + 1)
                for i in range(HB):
                    b = h * HB + i
                    m = pe_.matmul(ps[:, h, tok(i)], q1_t[:, tok(b)], k1_t[:, tok(b)], start=True, stop=True)
                m.then_inc(s1_mm, 1)
            for h in range(HALVES):
                pe_.wait_ge(p_done, h + 1)
                for i in range(HB):
                    t = pe_.transpose(ps[:, 2 + h, tok(i)], pr[:, h * HB + i, :], ident)
                t.then_inc(p_tr, 1)
            for h in range(HALVES):
                pe_.wait_ge(p_evac, h + 1)
                for i in range(HB):
                    b = h * HB + i
                    m = pe_.matmul(ps[:, 4 + h, tok(i)], pr_t[:, b, :], v1[:, b, :], start=True, stop=True)
                m.then_inc(av1_mm, 1)
            for h in range(HALVES):
                pe_.wait_ge(xn_ready, 3 * HALVES + h + 1)
                transpose_half(h, h)
            for h in range(HALVES):
                pe_.wait_ge(xn_t_ready, 3 * HALVES + h + 1)
                for i in range(HB):
                    m = pe_.matmul(ps[:, 2 + h, tok(i)], xn_t[:, tok(h * HB + i)], wf[:, 1, :], start=True, stop=True)
                m.then_inc(f_mm, 1)

        @block.vector
        def _(dve):
            chain = [0]

            def link(ins):
                chain[0] += 1
                ins.then_inc(vec, 1)
                dve.wait_ge(vec, chain[0])

            def statistics(src, bs):
                for b in bs:
                    s = dve.bn_stats(stats[:, b, :], src[:, b, :])
                link(s)
                for b in bs:
                    s = dve.bn_aggr(mv[:, b, :], stats[:, b, :])
                link(s)
                dve.tensor_scalar(var_eps[:, bs.start:bs.stop], mv[:, bs.start:bs.stop, 1:2]
                                  .rearrange("p b o -> p (b o)"), EPS, None, ALU.add).then_inc(var_ready, 1)

            def normalise(src, bs, n_rstd):
                dve.wait_ge(rstd_ready, n_rstd)
                for b in bs:
                    s = dve.tensor_scalar(xn[:, b, :], src[:, b, :], mv[:, b, 0:1], rstd[:, b:b + 1], ALU.subtract,
                                          ALU.mult)
                return s

            dve.wait_ge(x_in, 16)
            statistics(x0, range(B))
            dve.wait_ge(rstd_ready, 1)
            for h in range(HALVES):
                normalise(x0, range(h * HB, (h + 1) * HB), 1).then_inc(xn_ready, 1)
            for n in range(4):
                col = A_COL + (1 - n % 2)
                dve.wait_ge(part1, n + 1)
                wait(dve, part2, n - 1)
                r = rest[:, n % 2, :]
                dve.scalar_tensor_tensor(r, ps[:, n, :], wa[:, col:col + 1], parts[n][:, 0, :], ALU.add,
                                         ALU.subtract).then_inc(rest_ready, 1)
                dve.wait_ge(part2, n + 1)
                dve.tensor_tensor(parts[n][:, 2, :], r, parts[n][:, 1, :], ALU.subtract).then_inc(part3, 1)
            dve.wait_ge(row_in, 16)
            dve.wait_ge(xn_tr, HALVES)
            for n in range(4):
                dve.wait_ge(v_proj, n + 1)
                bank = ps[:, 6 + n % 2, :].rearrange("p (i w) -> p i w", i=2)
                bv = row_sb[:, D:3 * D]
                two = slice(2 * n, 2 * n + 2)
                dve.tensor_tensor(xn[:, two, :], bank[:, :, 0:D], bv[:, 0:D].unsqueeze(1).broadcast_to([P, 2, D]),
                                  ALU.add)
                dve.tensor_tensor(v1[:, two, :], bank[:, :, D:2 * D],
                                  bv[:, D:2 * D].unsqueeze(1).broadcast_to([P, 2, D]), ALU.add).then_inc(v_evac, 1)
            dve.wait_ge(tg_ready, 1)
            dve.scalar_tensor_tensor(x0[:, :, :], row_sb[:, 0:D].unsqueeze(1).broadcast_to([P, B, D]), tg[:, 0:1],
                                     x0[:, :, :], ALU.mult, ALU.add).then_inc(xb_ready, 1)

            for step in range(NG + AV_LAG + 6):
                j = step
                if j < NG:
                    b, g = divmod(j, GROUPS)
                    dve.wait_ge(s_ready, j + 1)
                    m = dve.tensor_reduce(negm[:, b % 2, g * GH:(g + 1) * GH],
                                          ps[:, j % 2, :].rearrange("p (i k) -> p i k", i=GH), AX, ALU.max,
                                          negate=True)
                    m.then_inc(max_done, 1)
                    if g == GROUPS - 1:
                        dve.wait_ge(max_done, j + 1)
                        wait(dve, t_ready, t_before_negm(b - 2) + 1 if b >= 2 else 0)
                        link(dve.tensor_copy(negm_parts[:, b % 2, 0:H], negm[:, b % 2, :]))
                        dve.tensor_tensor(negm_parts[:, b % 2, H:2 * H], negm[:, b % 2, :], negm_parts[:, b % 2, 0:H],
                                          ALU.subtract).then_inc(negm_ready, 1)
                j = step - ST_LAG - 1
                if 0 <= j < NG:
                    dve.wait_ge(exp_done, j + 1)
                    wait(dve, av_done, j - RING + 1)
                    if by_vec(j):
                        dve.tensor_tensor(p2[:, j % RING, :], pe[:, j % RING, :], p1[:, j % RING, :],
                                          ALU.subtract).then_inc(p2_vec, 1)
                    else:
                        dve.tensor_copy(p1[:, j % RING, :], pe[:, j % RING, :]).then_inc(p1_vec, 1)
                if step % GROUPS == 0:
                    b = step // GROUPS - 4
                    if 0 <= b < B:
                        dve.wait_ge(av_done, GROUPS * (b + 1))
                        wait(dve, t_ready, t_before_o(b - 2) + 1 if b >= 2 else 0)
                        o = ps[:, 4 + b % 2, 0:H * VC].rearrange("p (h v) -> p h v", h=H)
                        dve.tensor_reduce(o_sum[:, b % 2, :].rearrange("p (h d) -> p h d", h=H),
                                          o[:, :, 0:3 * HD].rearrange("p h (t d) -> p h d t", t=3), AX, ALU.add)
                        link(dve.reciprocal(den[:, b % 2, :], o[:, :, 3 * HD:VC].rearrange("p h v -> p (h v)")))
                        dve.tensor_tensor(o_nat[:, b % 2, :].rearrange("p (h d) -> p h d", h=H),
                                          o_sum[:, b % 2, :].rearrange("p (h d) -> p h d", h=H),
                                          den[:, b % 2, :].unsqueeze(2).broadcast_to([P, H, HD]),
                                          ALU.mult).then_inc(o_done, 1)
                if step % GROUPS == 3:
                    b = step // GROUPS - 4
                    if 0 <= b < B:
                        dve.wait_ge(o_proj, b + 1)
                        dve.wait_ge(xb_ready, 1)
                        dve.scalar_tensor_tensor(x1[:, b, :], ps[:, 7, 0:D], tg[:, 0:1], x0[:, b, :], ALU.mult,
                                                 ALU.add).then_inc(x1_done, 1)

            dve.wait_ge(x1_done, B)
            for h in range(HALVES):
                statistics(x1, range(h * HB, (h + 1) * HB))
            dve.memset(cand[:, :, 0:4], BIG)
            for h in range(HALVES):
                normalise(x1, range(h * HB, (h + 1) * HB), 2 + h).then_inc(xn_ready, 1)
            for h in range(HALVES):
                dve.wait_ge(xn_t_ready, HALVES + h + 1)
                dve.tensor_tensor(xl[:, half(h)], ps[:, h, :], xh[:, half(h)].bitcast(F32),
                                  ALU.subtract).then_inc(low_done, 1)
            for h in range(HALVES):
                dve.wait_ge(gate_mm, h + 1)
                dve.tensor_copy(raw[:, seqs(h), :], ps[:, 2 + h, 0:HB * E].rearrange("p (b e) -> p b e", b=HB))\
                    .then_inc(gate_evac, 1)
            dve.wait_ge(gate_evac, HALVES)

            def of_group(t):
                return t.rearrange("p b (g e) -> p (b g) e", g=G)

            link(dve.tensor_reduce(gmax[:, :, :].rearrange("p b g -> p (b g)"), of_group(raw[:, :, :]), AX, ALU.max))
            mine = gmax[:, :, :].unsqueeze(3).broadcast_to([P, B, G, G])
            other = gmax[:, :, :].unsqueeze(2).broadcast_to([P, B, G, G])
            lower = wb[:, W_LOW:W_LOW + G * G].rearrange("p (g o) -> p g o", g=G).unsqueeze(1)\
                .broadcast_to([P, B, G, G])
            dve.tensor_tensor(cmp_a[:, :, :, :], other, mine, ALU.is_gt)
            link(dve.tensor_tensor(cmp_b[:, :, :, :], other, mine, ALU.is_ge))
            link(dve.tensor_tensor(cmp_b[:, :, :, :], cmp_b[:, :, :, :], lower, ALU.mult))
            link(dve.tensor_tensor(cmp_a[:, :, :, :], cmp_a[:, :, :, :], cmp_b[:, :, :, :], ALU.max))
            link(dve.tensor_reduce(rank[:, :, :], cmp_a[:, :, :, :], AX, ALU.add))
            link(dve.tensor_scalar(rank[:, :, :], rank[:, :, :], 2.0, -BIG, ALU.is_ge, ALU.mult))
            link(dve.tensor_tensor(cand[:, :, 4:4 + E].rearrange("p b (g e) -> p b g e", g=G),
                                   raw[:, :, :].rearrange("p b (g e) -> p b g e", g=G),
                                   rank[:, :, :].unsqueeze(3).broadcast_to([P, B, G, EG]), ALU.add))
            for b in range(B):
                m = dve.max(top8[:, b, :], cand[:, b, :])
            link(m)
            for b in range(B):
                m = dve.match_replace(left[:, b, :], top8[:, b, :], cand[:, b, :], TAKEN)
            link(m)
            dve.wait_ge(gate_exp, HALVES)
            link(dve.tensor_scalar(sg[:, :, :], sg[:, :, :], 1.0, None, ALU.add))
            link(dve.reciprocal(sg[:, :, :], sg[:, :, :]))
            link(dve.tensor_scalar(left[:, :, 4:4 + E], left[:, :, 4:4 + E], (BIG + TAKEN) / 2, None, ALU.is_ge))
            link(dve.tensor_tensor(wts[:, :, :], left[:, :, 4:4 + E], sg[:, :, :], ALU.mult))
            link(dve.tensor_reduce(wsum[:, :], wts[:, :, :], AX, ALU.add))
            link(dve.reciprocal(wsum[:, :], wsum[:, :]))
            link(dve.tensor_scalar(wsum[:, :], wsum[:, :], ROUTE_SCALE / 2, None, ALU.mult))
            dve.tensor_tensor(wts[:, :, :], wts[:, :, :], wsum[:, :].unsqueeze(2).broadcast_to([P, B, E]),
                              ALU.mult).then_inc(wts_ready, 1)
            for h in range(HALVES):
                dve.wait_ge(wts_tr, h + 1)
                dve.tensor_copy(wt_t[:, half(h)], ps[0:E, 4 + h, :]).then_inc(wt_evac, 1)

            def product(e, s, h):
                u = 2 * e + h
                dve.wait_ge(act_t, u + 1)
                dve.scalar_tensor_tensor(uu[:, h, :], th[:, h, :], 1.0, a1[:, h, :], ALU.add,
                                         ALU.mult).then_inc(vec_u, 1)
                dve.wait_ge(c_ready, u + 1)
                wait(dve, mult_done, u - 1)
                dve.wait_ge(vec_u, u + 1)
                dve.scalar_tensor_tensor(h0[:, h, :], ps[:, 2 + h, :], bslot[:, s, 2:3], uu[:, h, :], ALU.add,
                                         ALU.mult).then_inc(h0_done, 1)

            def low_h(u, slot):
                dve.wait_ge(hi_done, u + 1)
                wait(dve, w2_done, u - RING + 1)
                dve.tensor_tensor(hl[:, slot, :], hw[:, slot, :], hh[:, slot, :].bitcast(F32),
                                  ALU.subtract).then_inc(lo_done, 1)

            def expert(e, s):
                for h in range(HALVES):
                    product(e, s, h)
                    low_h(2 * e + h - 2, 2 * (1 - s) + h)

            product(0, 0, 0)
            product(0, 0, 1)
            expert(1, 1)
            expert(2, 0)
            expert(3, 1)
            with dve.Fori(4, E - 1, 2) as e:
                expert(e, 0)
                expert(e + 1, 1)
            low_h(2 * E - 2, 2)
            low_h(2 * E - 1, 3)

            for h in range(HALVES):
                dve.wait_ge(y_tr, h + 1)
                link(dve.scalar_tensor_tensor(flat(x2[:, seqs(h), :]), ps[:, h, :], tg[:, 2:3],
                                              flat(x1[:, seqs(h), :]), ALU.mult, ALU.add))
                statistics(x2, range(h * HB, (h + 1) * HB))
            for h in range(HALVES):
                normalise(x2, range(h * HB, (h + 1) * HB), 4 + h).then_inc(xn_ready, 1)
            for h in range(HALVES):
                dve.wait_ge(s1_mm, h + 1)
                link(dve.tensor_reduce(negm1[:, 0, seqs(h)], ps[:, h, :].rearrange("p (b k) -> p b k", b=HB), AX,
                                       ALU.max, negate=True))
                dve.tensor_scalar(negm1[:, 1, seqs(h)], negm1[:, 0, seqs(h)], scale1, None,
                                  ALU.mult).then_inc(negm1_done, 1)
            for h in range(HALVES):
                dve.wait_ge(p_tr, h + 1)
                dve.tensor_copy(flat(pr_t[:, seqs(h), :]), ps[:, 2 + h, :]).then_inc(p_evac, 1)
            for h in range(HALVES):
                dve.wait_ge(p_done, h + 1)
                link(dve.reciprocal(den1[:, 1, seqs(h)], den1[:, 0, seqs(h)]))
                link(dve.tensor_scalar(den1[:, 1, seqs(h)], den1[:, 1, seqs(h)], tg[:, 1:2], None, ALU.mult))
            for h in range(HALVES):
                dve.wait_ge(av1_mm, h + 1)
                for b in range(h * HB, (h + 1) * HB):
                    m = dve.scalar_tensor_tensor(x3[:, b, :], ps[:, 4 + h, tok(b % HB)], den1[:, 1, b:b + 1],
                                                 x2[:, b, :], ALU.mult, ALU.add)
                link(m)
                statistics(x3, range(h * HB, (h + 1) * HB))
            for h in range(HALVES):
                normalise(x3, range(h * HB, (h + 1) * HB), 6 + h).then_inc(xn_ready, 1)
            for h in range(HALVES):
                dve.wait_ge(f_mm, h + 1)
                dve.tensor_tensor(ff[:, seqs(h), :], ps[:, 2 + h, :].rearrange("p (b d) -> p b d", b=HB),
                                  row_sb[:, 3 * D:4 * D].unsqueeze(1).broadcast_to([P, HB, D]),
                                  ALU.add).then_inc(f_add, 1)
            for h in range(HALVES):
                dve.wait_ge(f_tanh, h + 1)
                dve.scalar_tensor_tensor(x4[:, seqs(h), :], fft[:, seqs(h), :], tg[:, 3:4], x3[:, seqs(h), :],
                                         ALU.mult, ALU.add).then_inc(x4_done, 1)


def kernel(**inputs):
    import concourse.bacc as bacc
    from concourse.bass_utils import run_bass_kernel_spmd

    v = {name: np.asarray(a) for name, a in inputs.items()}

    def by_depth(a):
        return a.reshape(H, HD, -1).transpose(1, 0, 2).reshape(D, -1)

    low = np.tril(np.ones((G, G), np.float32), -1).reshape(1, G * G)
    arrays = {
        "x": v["x"],
        "ctx_t": v["ctx_1024"].reshape(T, D).T,
        "w_a": np.concatenate([
            by_depth(v["L0_xattn_wk"]).T, by_depth(v["L0_xattn_wq"]).T, np.eye(P, dtype=np.float32),
            by_depth(v["L0_xattn_bq"]), by_depth(v["L0_xattn_bk"]),
            v["L1_xattn_bq"][:, None], v["L1_xattn_bk"][:, None]], axis=1),
        "w_b": np.concatenate([
            v["L0_xattn_wv"].T, v["L1_xattn_Wv"], v["L0_xattn_wo"].T, v["L1_xattn_Wq"], v["L1_xattn_Wk"],
            v["L1_ffn_weight"].T, v["L1_ffn_aux_weight1"].T, v["L1_ffn_aux_weight2"], v["L0_ffn_Wg"].T,
            np.repeat(low, P, axis=0)], axis=1),
        "rows": np.concatenate([v["L0_xattn_bo"], v["L0_xattn_bv"], v["L1_xattn_bv"], v["L1_ffn_bias"]])[None],
        "gates": np.concatenate([v["g_xattn"], v["g_ffn"]])[None],
        "b2": v["L0_ffn_b2"],
        "w_big": np.concatenate([v[n].transpose(2, 0, 1) for n in ("L0_ffn_W1", "L0_ffn_W3", "L0_ffn_W2")], axis=2),
        "b_cols": np.stack([v["L0_ffn_b1"].T, v["L0_ffn_b3"].T], axis=2),
    }
    nc = bacc.Bacc("TRN2", target_bir_lowering=False, num_devices=1)
    args = []
    for name in arrays:
        arrays[name] = np.ascontiguousarray(arrays[name])
        args.append(nc.dram_tensor(name, arrays[name].shape, F32, kind="ExternalInput").ap())
    args.append(nc.dram_tensor("out", (B, P, D), F32, kind="ExternalOutput").ap())
    flamingo(nc, *args)
    done = run_bass_kernel_spmd(nc, [arrays], core_ids=[0])
    return done.results[0]["out"]
```

```python
import numpy as np

import concourse.bass as bass
from concourse import mybir
from contextlib import ExitStack

F32 = mybir.dt.float32
F32R = mybir.dt.float32r
BF16 = mybir.dt.bfloat16
F16 = mybir.dt.float16
U32 = mybir.dt.uint32
ALU = mybir.AluOpType
ACT = mybir.ActivationFunctionType
AX = mybir.AxisListType.X

P = 128
D = 128
B = 8
HALVES = 2
HB = B // HALVES
HT = HB * P
T = B * P
H = 16
HD = D // H
E = 16
G = 4
EG = E // G
EPS = 1e-5
ROUTE_SCALE = 2.5
BIG = 3.0e38
TAKEN = 3.3e38

A_WK, A_WQ, A_ID, A_COL = 0, D, 2 * D, 3 * D
A_W = 3 * D + 4
(W_V, W_O, W_Q1, W_K1, W_F, W_A1, W_A2, W_G, W_LOW) = (0, 256, 384, 512, 640, 768, 896, 1024, 1024 + E)
B_W = W_LOW + G * G

Q_PARTS = (0, 0, 0, 1, 1, 2)
K_PARTS = (0, 1, 2, 0, 1, 0)
MAX_ROW = HD * len(Q_PARTS)

TWO_ONES = 0x3F803F80

GROUPS = 4
GH = H // GROUPS
NG = B * GROUPS
ST_LAG = 9
AV_LAG = ST_LAG + 3
VC = 3 * HD + 1
RING = 4
SETS = (range(0, HB), range(HB, HB + 2), range(HB + 2, B))
STEPS = NG + AV_LAG + GROUPS
EARLY = 2
CHUNKS = ((0, 2), (2, 5), (5, 10), (10, 16))
STEP_EXP = 42
STEP_N2 = 32
HRING = 4
WEB = 4
AHEAD = 2


def flamingo(nc, x, ctx_t, w_a, w_b, rows, gates, b2, w_big, b_cols, out):
    scale0 = float(HD) ** -0.5
    scale1 = float(D) ** -0.5
    web_dram = nc.dram_tensor("web_dram", [E, T], F32, kind="Internal").ap()

    stack = ExitStack()
    with stack:
        def sb(name, shape, dt=F32):
            return stack.enter_context(nc.sbuf_tensor(name, shape, dt))

        def sem(name):
            return stack.enter_context(nc.semaphore(name))

        def set_seqs(k):
            return slice(SETS[k].start, SETS[k].stop)

        def set_tok(k):
            return slice(SETS[k].start * P, SETS[k].stop * P)

        def set_cols(k):
            return slice(0, len(SETS[k]) * P)

        def norm_range(norm, k):
            return seqs_range(k) if norm == 2 else SETS[k]

        def flat(ap):
            return ap.rearrange("p b t -> p (b t)")

        x0 = sb("x0", [P, B, D])
        x1 = sb("x1", [P, B, D])
        x2 = x0
        x3 = x1
        xn = sb("xn", [P, B, D])
        xn_t = sb("xn_t", [P, T])
        xh = sb("xh", [P, T], F32R)
        xl = sb("xl", [P, T], F32R)
        ctx_sb = sb("ctx_sb", [P, T])
        wa = sb("wa", [P, A_W])
        wb = sb("wb", [P, B_W])
        row_sb = sb("row_sb", [P, 4 * D])
        gate_sb = sb("gate_sb", [P, 4])
        tg = sb("tg", [P, 4])
        b2_sb = sb("b2_sb", [E, D])
        b2_twice = sb("b2_twice", [E, D])
        wh = sb("wh", [P, E, 3 * D], F32R)
        wl = sb("wl", [P, E, 3 * D], F32R)
        bcol = sb("bcol", [P, E, 3])
        stats = sb("stats", [P, B, 6])
        mv = sb("mv", [P, B, 2])
        var_eps = sb("var_eps", [P, B])
        rstd = sb("rstd", [P, B])
        minus_half = sb("minus_half", [P, B])
        identb = sb("identb", [P, P], BF16)
        rest = x1[:, :, :].rearrange("p b d -> p (b d)").rearrange("p (s t) -> p s t", s=2)
        qs = sb("qs", [P, H, T], BF16)
        ks = sb("ks", [P, H, T], BF16)
        v_parts = sb("v_parts", [P, B * H, VC], BF16)
        v1 = sb("v1", [P, B, D])
        k1_t = sb("k1_t", [P, T])
        negm = sb("negm", [P, 2, H])
        negm_parts = sb("negm_parts", [P, 2, 2 * H], BF16)
        negm_rows = sb("negm_rows", [2 * H, 2, P], BF16)
        o_sum = sb("o_sum", [P, 2, D])
        o_nat = sb("o_nat", [P, 2, D])
        o_t = sb("o_t", [P, 2, P])
        den = sb("den", [P, 2, H])
        wf = sb("wf", [P, 2, D])
        raw = sb("raw", [P, B, E])
        sg = sb("sg", [P, B, E])
        gmax = sb("gmax", [P, B, G])
        cmp_a = sb("cmp_a", [P, B, G, G])
        cmp_b = sb("cmp_b", [P, B, G, G])
        rank = sb("rank", [P, B, G])
        cand = sb("cand", [P, B, 4 + E])
        top8 = sb("top8", [P, B, 8])
        left = sb("left", [P, B, 4 + E])
        wts = sb("wts", [P, B, E])
        wsum = sb("wsum", [P, B])
        wt_t = sb("wt_t", [E, T])
        with ExitStack() as first:
            def once(name, shape, dt=F32):
                return first.enter_context(nc.sbuf_tensor(name, shape, dt))

            pe = once("pe", [P, RING, GH * P])
            pe_free = flat(pe[:, :, :]).bitcast(BF16)
            parts = [once(f"parts{n}", [P, 3, HT], BF16) for n in range(2)]
            parts += [pe_free[:, n * 3 * HT:(n + 1) * 3 * HT].rearrange("p (s t) -> p s t", s=3) for n in range(2)]
            p1 = once("p1", [P, RING, GH * P], F16)
            p2 = once("p2", [P, RING, GH * P], F16)
        hh = sb("hh", [P, HRING, HT], F32R)
        hl = sb("hl", [P, HRING, HT], F32R)
        qs_free = qs[:, :, :].rearrange("p h t -> p (h t)").bitcast(F32)
        a1, th, uu, h0 = (qs_free[:, n * T:(n + 1) * T].rearrange("p (s t) -> p s t", s=2) for n in range(4))
        web, hw = (qs_free[:, n * T:(n + 2) * T].rearrange("p (s t) -> p s t", s=4) for n in (4, 6))
        ks_free = ks[:, :, :].rearrange("p h t -> p (h t)").bitcast(F32)
        y_t, q1_t, pr, pr_t, ff, fft, x4 = (ks_free[:, n * T:(n + 1) * T] for n in range(7))
        pr, pr_t, ff, fft, x4 = (t.rearrange("p (b t) -> p b t", b=B) for t in (pr, pr_t, ff, fft, x4))
        w_first = ctx_sb[:, 0:EARLY * 3 * D].rearrange("p (e w) -> p e w", e=EARLY)
        w_rest = ks_free[:, 0:(E - EARLY) * 3 * D].rearrange("p (e w) -> p e w", e=E - EARLY)
        negm1 = sb("negm1", [P, 2, B])
        den1 = sb("den1", [P, 2, B])

        ps = stack.enter_context(nc.psum_tensor("ps", [P, 8, 512], F32))
        ident = wa[:, A_ID:A_ID + P]

        x_in, ctx_in, wa_in, wb_in, row_in, gate_in, b2_in, bcol_in = (
            sem(n) for n in ("x_in", "ctx_in", "wa_in", "wb_in", "row_in", "gate_in", "b2_in", "bcol_in"))
        rows_in = [sem(f"rows_in{n}") for n in range(4)]
        negm_in = [sem(f"negm_in{n}") for n in range(2)]
        web_in = [sem(f"web_in{n}") for n in range(WEB)]
        raw_in = [sem(f"raw_in{n}") for n in range(len(CHUNKS))]
        wt_out = sem("wt_out")
        out_done = sem("out_done")
        vec = sem("vec")
        vec_u = sem("vec_u")
        pads, pools_ready = sem("pads"), sem("pools_ready")
        var_ready, rstd_ready, xn_ready, xn_tr, xn_t_ready = (
            sem(n) for n in ("var_ready", "rstd_ready", "xn_ready", "xn_tr", "xn_t_ready"))
        proj_ready, part1, rest_ready, part2, part3 = (
            sem(n) for n in ("proj_ready", "part1", "rest_ready", "part2", "part3"))
        v_proj, v_evac, v_part1, v_rest, v_part2, v_done = (
            sem(n) for n in ("v_proj", "v_evac", "v_part1", "v_rest", "v_part2", "v_done"))
        k1_proj, k1_evac, wf_mm, wf_evac, tg_ready, identb_ready, xb_ready, bcol_ready = (
            sem(n) for n in ("k1_proj", "k1_evac", "wf_mm", "wf_evac", "tg_ready", "identb_ready", "xb_ready",
                             "bcol_ready"))
        s_ready, max_done, negm_ready, t_ready, t_evac = (
            sem(n) for n in ("s_ready", "max_done", "negm_ready", "t_ready", "t_evac"))
        st_ready, exp_done, p2_pool, p2_vec, av_done = (
            sem(n) for n in ("st_ready", "exp_done", "p2_pool", "p2_vec", "av_done"))
        o_done, o_proj, x1_done = (sem(n) for n in ("o_done", "o_proj", "x1_done"))
        x_split, gate_mm, gate_evac, gate_exp, wts_ready, wts_tr, wt_evac, b2_ready, b2_mm, low_done = (
            sem(n) for n in ("x_split", "gate_mm", "gate_evac", "gate_exp", "wts_ready", "wts_tr", "wt_evac",
                             "b2_ready", "b2_mm", "low_done"))
        a_ready, c_ready, act_t, h0_done, mult_done, hi_done, w2_done = (
            sem(n) for n in ("a_ready", "c_ready", "act_t", "h0_done", "mult_done", "hi_done", "w2_done"))
        lo_done = [sem(f"lo_done{n}") for n in range(2)]
        w_hi, w13_lo, w2_lo = (sem(n) for n in ("w_hi", "w13_lo", "w2_lo"))
        y_evac, y_tr, q1_mm, q1_evac, s1_mm, negm1_done, p_done, p_tr, p_evac, av1_mm, f_mm, f_add, f_tanh, x4_done = (
            sem(n) for n in ("y_evac", "y_tr", "q1_mm", "q1_evac", "s1_mm", "negm1_done", "p_done", "p_tr", "p_evac",
                             "av1_mm", "f_mm", "f_add", "f_tanh", "x4_done"))

        def wait(eng, s, count):
            if not isinstance(count, int) or count > 0:
                eng.wait_ge(s, count)

        def tok(b):
            return slice(b * P, (b + 1) * P)

        def half(h):
            return slice(h * HT, (h + 1) * HT)

        def seqs(h):
            return slice(h * HB, (h + 1) * HB)

        def seqs_range(h):
            return range(h * HB, (h + 1) * HB)

        def w_of(e):
            if isinstance(e, int) and e < EARLY:
                return w_first[:, e:e + 1, :]
            return w_rest[:, bass.ds(e - EARLY, 1), :]

        def by_vec(j):
            return j % GROUPS == GROUPS - 1

        def wait_p2(eng, j):
            if j >= 0:
                if by_vec(j):
                    eng.wait_ge(p2_vec, j // GROUPS + 1)
                else:
                    eng.wait_ge(p2_pool, j - j // GROUPS + 1)

        def t_before_negm(b):
            return b + max(0, b - 3)

        def t_before_o(b):
            return min(B, b + 4) + b

        NORMS = [(2, 0), (2, 1), (3, 0), (4, 0), (3, 1), (3, 2), (4, 1), (4, 2)]

        def norm_count(norm, h):
            return NORMS.index((norm, h)) + 1

        def stage_bank(stage, k):
            n = ("experts", "norm 3", "queries", "scores", "probabilities", "values", "norm 4", "last").index(stage)
            return (6, 0, 2)[k] + n % 2

        def norm_bank(norm, h):
            return (0, 6)[h] if norm == 2 else stage_bank(f"norm {norm}", h)

        def gate_bank(h):
            return (1, 7)[h]

        def wts_bank(h):
            return (0, 6)[h]

        block = stack.enter_context(nc.Block())

        @block.sync
        def _(sp):
            sp.dma_start(x0[:, :, :], x.rearrange("b t d -> t b d")).then_inc(x_in, 16)
            sp.dma_start(ctx_sb[:, :], ctx_t).then_inc(ctx_in, 16)
            sp.dma_start(wa[:, :], w_a).then_inc(wa_in, 16)
            sp.dma_start(wb[:, :], w_b).then_inc(wb_in, 16)
            sp.dma_start(row_sb[:, :], rows.partition_broadcast(P)).then_inc(row_in, 16)
            sp.dma_start(gate_sb[:, :], gates.partition_broadcast(P)).then_inc(gate_in, 16)
            for n in range(4):
                dst, terms = (qs, Q_PARTS) if n % 2 else (ks, K_PARTS)
                sp.wait_ge(pads, n + 1)
                for part, ready in enumerate((part1, part2, part3)):
                    sp.wait_ge(ready, n + 1)
                    for r, term in enumerate(terms):
                        if term == part:
                            sp.dma_start(dst[r * HD:(r + 1) * HD, :, half(n // 2)],
                                         parts[n][:, part, :]).then_inc(rows_in[n], 16)
            sp.dma_start(b2_sb[:, :], b2).then_inc(b2_in, 16)
            sp.dma_start(bcol[:, :, 1:3], b_cols).then_inc(bcol_in, 16)

            def bring_weights(c):
                lo, hi = CHUNKS[c]
                dst = w_first if c == 0 else w_rest[:, lo - EARLY:hi - EARLY, :]
                sp.dma_start(dst, w_big[:, lo:hi, :]).then_inc(raw_in[c], 16)

            sp.wait_ge(v_proj, 4)
            sp.wait_ge(k1_proj, 2)
            bring_weights(0)
            for b in range(B):
                sp.wait_ge(t_evac, t_before_negm(b) + 1)
                sp.dma_start(qs[MAX_ROW:MAX_ROW + 2, :, tok(b)], negm_rows[:, b % 2, :]).then_inc(negm_in[b % 2], 16)
            def store_weights(h):
                sp.wait_ge(wt_evac, h + 1)
                sp.dma_start(web_dram[:, half(h)], wt_t[:, half(h)]).then_inc(wt_out, 16)
                sp.wait_ge(wt_out, 16 * (h + 1))

            def spread(u, e, s, h):
                wait(sp, mult_done, u - (WEB - 1))
                sp.dma_start(web[:, s, :], web_dram[bass.ds(e, 1), half(h)].partition_broadcast(P))\
                    .then_inc(web_in[s], 16)

            sp.wait_ge(st_ready, NG)
            bring_weights(1)
            store_weights(0)
            for s in range(WEB):
                spread(s, s, s, 0)
            bring_weights(2)
            bring_weights(3)
            with sp.Fori(WEB, E - WEB + 1, WEB) as e:
                for s in range(WEB):
                    spread(e + s, e + s, s, 0)
            store_weights(1)
            with sp.Fori(0, E - WEB + 1, WEB) as e:
                for s in range(WEB):
                    spread(e + (E + s), e + s, s, 1)
            out_t = out.rearrange("b t d -> t b d")
            for k in range(len(SETS)):
                sp.wait_ge(x4_done, k + 1)
                sp.dma_start(out_t[:, set_seqs(k), :], x4[:, set_seqs(k), :]).then_inc(out_done, 16)
            sp.wait_ge(out_done, 16 * len(SETS))

        @block.gpsimd
        def _(pool):
            pool.memset(minus_half[:, :], -0.5).then_inc(pools_ready, 1)
            pool.memset(ks[:, :, 0:HT].bitcast(U32), TWO_ONES).then_inc(pads, 1)
            pool.memset(qs[:, :, 0:HT].bitcast(U32), 0).then_inc(pads, 1)
            pool.wait_ge(pools_ready, 1)
            pool.wait_ge(var_ready, 1)
            pool.tensor_tensor(rstd[:, :], var_eps[:, :], minus_half[:, :], ALU.pow).then_inc(rstd_ready, 1)
            pool.memset(ks[:, :, HT:T].bitcast(U32), TWO_ONES).then_inc(pads, 1)
            pool.memset(qs[:, :, HT:T].bitcast(U32), 0).then_inc(pads, 1)
            pool.memset(v_parts[:, :, VC - 1:VC], 1.0).then_inc(pools_ready, 1)
            for h in range(HALVES):
                hv = slice(h * HB * H, (h + 1) * HB * H)
                vf = flat(xn[:, seqs(h), :]).rearrange("p (n d) -> p n d", d=HD)
                pool.wait_ge(v_part1, h + 1)
                pool.tensor_tensor(vf, vf, v_parts[:, hv, 2 * HD:3 * HD], ALU.subtract).then_inc(v_rest, 1)
                pool.wait_ge(v_part2, h + 1)
                pool.tensor_tensor(v_parts[:, hv, 0:HD], vf, v_parts[:, hv, HD:2 * HD], ALU.subtract).then_inc(v_done, 1)
            def root(norm, k):
                bs = norm_range(norm, k)
                pool.wait_ge(var_ready, 1 + norm_count(norm, k))
                pool.tensor_tensor(rstd[:, bs.start:bs.stop], var_eps[:, bs.start:bs.stop],
                                   minus_half[:, bs.start:bs.stop], ALU.pow).then_inc(rstd_ready, 1)

            def split13(e):
                pool.wait_ge(w_hi, e + 1)
                pool.tensor_tensor(wl[:, bass.ds(e, 1), 0:2 * D], w_of(e)[:, :, 0:2 * D],
                                   wh[:, bass.ds(e, 1), 0:2 * D].bitcast(F32), ALU.subtract).then_inc(w13_lo, 1)

            for j in range(NG):
                if j == STEP_N2 - ST_LAG:
                    root(2, 0)
                if j in (NG - 6, NG - 2):
                    split13(0 if j == NG - 6 else 1)
                if not by_vec(j):
                    pool.wait_ge(exp_done, j + 1)
                    wait(pool, av_done, j - RING + 1)
                    pool.tensor_tensor(p2[:, j % RING, :], pe[:, j % RING, :], p1[:, j % RING, :],
                                       ALU.subtract).then_inc(p2_pool, 1)

            def weight(u, s, w):
                pool.wait_ge(web_in[w], (u - w) * (16 // WEB) + 16)
                pool.wait_ge(h0_done, u + 1)
                if not isinstance(u, int) or u >= HRING:
                    pool.wait_ge(lo_done[s], u - HRING + 2 - s)
                pool.tensor_tensor(hw[:, w, :], h0[:, s, :], web[:, w, :], ALU.mult).then_inc(mult_done, 1)

            def low_h(u, w):
                pool.wait_ge(hi_done, u + 1)
                pool.tensor_tensor(hl[:, w, :], hw[:, w, :], hh[:, w, :].bitcast(F32),
                                   ALU.subtract).then_inc(lo_done[1], 2)

            for u in range(2 * E):
                if EARLY <= u + AHEAD < E:
                    split13(u + AHEAD)
                if u >= 4 and u % 2 == 0:
                    low_h(u - 3, (u - 3) % HRING)
                weight(u, u % 2, u % WEB)
                if u == 1:
                    root(2, 1)
                if u == E + 5:
                    root(3, 0)
            for norm, k in NORMS[3:]:
                root(norm, k)

        @block.scalar
        def _(act):
            act.wait_ge(gate_in, 16)
            act.activation(tg[:, :], gate_sb[:, :], ACT.Tanh).then_inc(tg_ready, 1)
            act.wait_ge(wa_in, 16)
            act.activation(identb[:, :], ident, ACT.Copy).then_inc(identb_ready, 1)

            def first_part(n):
                col = A_COL + (1 - n % 2)
                act.wait_ge(proj_ready, n + 1)
                act.activation(parts[n][:, 0, :], ps[:, n, :], ACT.Identity, bias=wa[:, col:col + 1]).then_inc(part1, 1)

            def second_part(n):
                act.wait_ge(rest_ready, n + 1)
                act.activation(parts[n][:, 1, :], rest[:, n % 2, :], ACT.Copy).then_inc(part2, 1)

            for h in range(HALVES):
                first_part(2 * h)
                act.wait_ge(xn_tr, h + 1)
                act.activation(xn_t[:, half(h)], ps[:, 4 + h, :], ACT.Copy).then_inc(xn_t_ready, 1)
                second_part(2 * h)
                first_part(2 * h + 1)
                second_part(2 * h + 1)
            act.wait_ge(pools_ready, 2)
            for h in range(HALVES):
                hv = slice(h * HB * H, (h + 1) * HB * H)
                vf = flat(xn[:, seqs(h), :]).rearrange("p (n d) -> p n d", d=HD)
                act.wait_ge(v_evac, 2 * h + 2)
                act.activation(v_parts[:, hv, 2 * HD:3 * HD], vf, ACT.Copy).then_inc(v_part1, 1)
                act.wait_ge(v_rest, h + 1)
                act.activation(v_parts[:, hv, HD:2 * HD], vf, ACT.Copy).then_inc(v_part2, 1)
            for h in range(HALVES):
                act.wait_ge(k1_proj, h + 1)
                act.activation(k1_t[:, half(h)], ps[:, 4 + h, :], ACT.Identity,
                               bias=wa[:, A_COL + 3:A_COL + 4]).then_inc(k1_evac, 1)
            for n in range(2):
                act.wait_ge(wf_mm, n + 1)
                act.activation(wf[:, n, :], ps[:, 7, 0:D], ACT.Copy).then_inc(wf_evac, 1)
            act.wait_ge(bcol_in, 16)
            act.activation(bcol[:, :, 0:1], bcol[:, :, 1:2], ACT.Copy, scale=0.5).then_inc(bcol_ready, 1)
            act.wait_ge(b2_in, 16)
            act.activation(b2_twice[:, :], b2_sb[:, :], ACT.Copy, scale=2.0).then_inc(b2_ready, 1)

            def norm_out(norm, k):
                bs = norm_range(norm, k)
                columns, src = slice(bs.start * P, bs.stop * P), ps[:, norm_bank(norm, k), 0:len(bs) * P]
                act.wait_ge(xn_tr, HALVES + norm_count(norm, k))
                if norm == 2:
                    act.activation(xh[:, columns], src, ACT.Copy)
                act.activation(xn_t[:, columns], src, ACT.Copy).then_inc(xn_t_ready, 1)

            def gate_exponential(h):
                act.wait_ge(gate_evac, h + 1)
                act.activation(sg[:, seqs(h), :], raw[:, seqs(h), :], ACT.Exp, scale=-1.0).then_inc(gate_exp, 1)

            def high_w(e):
                if isinstance(e, int):
                    act.wait_ge(raw_in[[e < hi for lo, hi in CHUNKS].index(True)], 16)
                act.activation(wh[:, bass.ds(e, 1), :], w_of(e), ACT.Copy).then_inc(w_hi, 1)

            def high_h(u):
                w = u % HRING
                act.wait_ge(mult_done, u + 1)
                wait(act, w2_done, u - (HRING - 1))
                act.activation(hh[:, w, :], hw[:, w, :], ACT.Copy).then_inc(hi_done, 1)

            def first_product(u, e, s):
                act.wait_ge(a_ready, u + 1)
                wait(act, h0_done, u - 1)
                act.activation(a1[:, s, :], ps[:, s, :], ACT.Identity,
                               bias=bcol[:, bass.ds(e, 1), 1:2].rearrange("p e o -> p (e o)"))
                act.activation(th[:, s, :], ps[:, s, :], ACT.Tanh, scale=0.5,
                               bias=bcol[:, bass.ds(e, 1), 0:1].rearrange("p e o -> p (e o)")).then_inc(act_t, 1)

            act.wait_ge(rows_in[2], 16 * len(K_PARTS))
            act.wait_ge(rows_in[3], 16 * len(Q_PARTS))
            for step in range(STEPS):
                if step == STEP_N2 + 2:
                    norm_out(2, 0)
                if step == STEP_N2 + 4:
                    gate_exponential(0)
                if step in (STEP_EXP - 6, STEP_EXP - 4):
                    high_w(0 if step == STEP_EXP - 6 else 1)
                j = step - ST_LAG
                if 0 <= j < NG:
                    act.wait_ge(st_ready, j + 1)
                    wait_p2(act, j - RING)
                    act.activation(pe[:, j % RING, :], ps[:, 2 + j % 2, :], ACT.Exp, scale=scale0)
                    wait(act, av_done, j - RING + 1)
                    act.activation(p1[:, j % RING, :], ps[:, 2 + j % 2, :], ACT.Exp, scale=scale0).then_inc(exp_done, 1)
                if step % GROUPS == 1:
                    b = step // GROUPS - 1
                    if 0 <= b < B:
                        act.wait_ge(t_ready, t_before_negm(b) + 1)
                        if b >= 2:
                            act.wait_ge(negm_in[b % 2], 16 * (b // 2))
                        act.activation(negm_rows[:, b % 2, :], ps[0:2 * H, 6, 0:P // 2].bitcast(BF16),
                                       ACT.Copy).then_inc(t_evac, 1)
                    b = step // GROUPS - 4
                    if 0 <= b < B:
                        act.wait_ge(t_ready, t_before_o(b) + 1)
                        wait(act, o_proj, b - 1)
                        act.activation(o_t[:, b % 2, :], ps[:, 6, 0:P], ACT.Copy).then_inc(t_evac, 1)
                if step in (STEP_EXP + 1, STEP_EXP + 3):
                    u = (step - STEP_EXP - 1) // 2
                    high_w(u + AHEAD)
                    first_product(u, u, u)
            def y_out(k):
                h, first = divmod(SETS[k].start, HB)
                act.wait_ge(w2_done, E * (h + 1))
                act.activation(y_t[:, set_tok(k)], ps[:, 4 + h, first * P:(first + len(SETS[k])) * P],
                               ACT.Copy).then_inc(y_evac, 1)

            def queries(k):
                act.wait_ge(q1_mm, k + 1)
                act.activation(q1_t[:, set_tok(k)], ps[:, stage_bank("queries", k), set_cols(k)], ACT.Identity,
                               bias=wa[:, A_COL + 2:A_COL + 3]).then_inc(q1_evac, 1)

            def exponentials(k):
                act.wait_ge(negm1_done, k + 1)
                for i, b in enumerate(SETS[k]):
                    e = act.activation(pr[:, b, :], ps[:, stage_bank("scores", k), tok(i)], ACT.Exp, scale=scale1,
                                       bias=negm1[:, 1, b:b + 1], accum_out=den1[:, 0, b:b + 1])
                e.then_inc(p_done, 1)

            def last_tanh(k):
                act.wait_ge(f_add, k + 1)
                act.activation(fft[:, set_seqs(k), :], ff[:, set_seqs(k), :], ACT.Tanh).then_inc(f_tanh, 1)

            for u in range(EARLY, 2 * E):
                if u + AHEAD < E:
                    high_w(u + AHEAD)
                if u >= 3:
                    high_h(u - 3)
                first_product(u, u % E, u % 2)
                if u == 4:
                    norm_out(2, 1)
                if u == 7:
                    gate_exponential(1)
                if u == E + 3:
                    y_out(0)
                if u == E + 9:
                    norm_out(3, 0)
                if u == E + 11:
                    queries(0)
                if u == E + 14:
                    exponentials(0)
            for u in range(2 * E - 3, 2 * E):
                high_h(u)
            late = (1, 2)
            for k in late:
                y_out(k)
            norm_out(4, 0)
            for k in late:
                norm_out(3, k)
            for k in late:
                queries(k)
            last_tanh(0)
            for k in late:
                exponentials(k)
            for k in late:
                norm_out(4, k)
            for k in late:
                last_tanh(k)

        @block.tensor
        def _(pe_):
            def norm_turn(norm, k):
                pe_.wait_ge(xn_ready, HALVES + norm_count(norm, k))
                turn_sequences(norm_range(norm, k), norm_bank(norm, k))

            def gate_scores(h):
                pe_.wait_ge(xn_t_ready, HALVES + norm_count(2, h))
                for i in range(HB):
                    m = pe_.matmul(ps[:, gate_bank(h), i * E:(i + 1) * E], xn_t[:, tok(h * HB + i)],
                                   wb[:, W_G:W_G + E], start=True, stop=True)
                m.then_inc(gate_mm, 1)

            def turn_weights(h):
                pe_.wait_ge(wts_ready, h + 1)
                pe_.wait_ge(low_done, h + 1)
                for i in range(HB):
                    t = pe_.transpose(ps[0:E, wts_bank(h), tok(i)], wts[:, h * HB + i, :], ident)
                t.then_inc(wts_tr, 1)

            def turn_sequences(bs, bank):
                for i, b in enumerate(bs):
                    t = pe_.transpose(ps[:, bank, tok(i)], xn[:, b, :], ident)
                t.then_inc(xn_tr, 1)

            pe_.wait_ge(ctx_in, 16)
            pe_.wait_ge(wa_in, 16)
            for h in range(HALVES):
                pe_.matmul(ps[:, 2 * h, :], wa[:, A_WK:A_WK + D], ctx_sb[:, half(h)], start=True,
                           stop=True).then_inc(proj_ready, 1)
                pe_.wait_ge(xn_ready, h + 1)
                turn_sequences(seqs_range(h), 4 + h)
                pe_.wait_ge(xn_t_ready, h + 1)
                pe_.matmul(ps[:, 2 * h + 1, :], wa[:, A_WQ:A_WQ + D], xn_t[:, half(h)], start=True,
                           stop=True).then_inc(proj_ready, 1)
            pe_.wait_ge(wb_in, 16)
            for n in range(4):
                wait(pe_, v_evac, n - 1)
                for i in range(2):
                    m = pe_.matmul(ps[:, 6 + n % 2, i * 2 * D:(i + 1) * 2 * D], ctx_sb[:, tok(2 * n + i)],
                                   wb[:, W_V:W_V + 2 * D], start=True, stop=True)
                m.then_inc(v_proj, 1)
            for h in range(HALVES):
                pe_.matmul(ps[:, 4 + h, :], wb[:, W_K1:W_K1 + D], ctx_sb[:, half(h)], start=True,
                           stop=True).then_inc(k1_proj, 1)
            pe_.wait_ge(v_evac, 4)
            pe_.matmul(ps[:, 7, 0:D], wb[:, W_A1:W_A1 + D], wb[:, W_A2:W_A2 + D], start=True,
                       stop=True).then_inc(wf_mm, 1)
            pe_.wait_ge(wf_evac, 1)
            pe_.matmul(ps[:, 7, 0:D], wb[:, W_F:W_F + D], wf[:, 0, :], start=True, stop=True).then_inc(wf_mm, 1)

            def up(u):
                h, e = divmod(u, E)
                wait(pe_, w13_lo, min(u, E - 1) + 1)
                for bank, col, freed, ready in ((u % 2, 0, act_t, a_ready), (2 + u % 2, D, h0_done, c_ready)):
                    wait(pe_, freed, u - 1)
                    cols = slice(col, col + D)
                    pe_.matmul(ps[:, bank, :], wh[:, e, cols], xh[:, half(h)], start=True, stop=False)
                    pe_.matmul(ps[:, bank, :], wh[:, e, cols], xl[:, half(h)], start=False, stop=False)
                    pe_.matmul(ps[:, bank, :], wl[:, e, cols], xh[:, half(h)], start=False,
                               stop=True).then_inc(ready, 1)

            pe_.wait_ge(identb_ready, 1)
            pe_.wait_ge(rest_ready, 4)
            pe_.wait_ge(wf_evac, 2)
            pe_.wait_ge(k1_evac, 2)
            for step in range(STEPS):
                if step == STEP_N2 + 2:
                    pe_.wait_ge(max_done, NG)
                    norm_turn(2, 0)
                if step == STEP_N2 + 3:
                    gate_scores(0)
                if step == STEP_N2 + 8:
                    turn_weights(0)
                j = step
                if j < NG:
                    b, g = divmod(j, GROUPS)
                    if j % (GROUPS * HB) == 0:
                        for n in (0, 1):
                            pe_.wait_ge(rows_in[2 * (b // HB) + n], 16 * len(Q_PARTS))
                    wait(pe_, max_done, j - 1)
                    for i in range(GH):
                        m = pe_.matmul(ps[:, j % 2, tok(i)], qs[:, g * GH + i, tok(b)], ks[:, g * GH + i, tok(b)],
                                       start=True, stop=True)
                    m.then_inc(s_ready, 1)
                j = step - ST_LAG
                if 0 <= j < NG:
                    b, g = divmod(j, GROUPS)
                    if g == 0:
                        pe_.wait_ge(negm_in[b % 2], 16 * (b // 2 + 1))
                    wait(pe_, exp_done, j - 1)
                    for i in range(GH):
                        m = pe_.matmul(ps[:, 2 + j % 2, tok(i)], ks[:, g * GH + i, tok(b)], qs[:, g * GH + i, tok(b)],
                                       start=True, stop=True)
                    m.then_inc(st_ready, 1)
                j = step - AV_LAG
                if 0 <= j < NG:
                    b, g = divmod(j, GROUPS)
                    if j % (GROUPS * HB) == 0:
                        pe_.wait_ge(v_done, b // HB + 1)
                    if g == 0:
                        wait(pe_, o_done, b - 1)
                    wait_p2(pe_, j)
                    for i in range(GH):
                        hd = g * GH + i
                        pe_.matmul(ps[:, 4 + b % 2, hd * VC:(hd + 1) * VC], p1[:, j % RING, tok(i)],
                                   v_parts[:, b * H + hd, :], start=True, stop=True)
                        m = pe_.matmul(ps[:, 4 + b % 2, hd * VC + HD:(hd + 1) * VC], p2[:, j % RING, tok(i)],
                                       v_parts[:, b * H + hd, HD:VC], start=False, stop=True, skip_group_check=True)
                    m.then_inc(av_done, 1)
                if step % GROUPS == 1:
                    b = step // GROUPS - 1
                    if 0 <= b < B:
                        pe_.wait_ge(negm_ready, b + 1)
                        wait(pe_, t_evac, t_before_negm(b))
                        pe_.transpose(ps[0:2 * H, 6, 0:P // 2].bitcast(BF16), negm_parts[:, b % 2, :],
                                      identb[:, :]).then_inc(t_ready, 1)
                    b = step // GROUPS - 4
                    if 0 <= b < B:
                        pe_.wait_ge(o_done, b + 1)
                        wait(pe_, t_evac, t_before_o(b))
                        pe_.transpose(ps[:, 6, 0:P], o_nat[:, b % 2, :], ident).then_inc(t_ready, 1)
                if step % GROUPS == 2:
                    b = step // GROUPS - 4
                    if 0 <= b < B:
                        pe_.wait_ge(t_evac, t_before_o(b) + 1)
                        wait(pe_, x1_done, b)
                        pe_.matmul(ps[:, 7, 0:D], o_t[:, b % 2, :], wb[:, W_O:W_O + D], start=True,
                                   stop=True).then_inc(o_proj, 1)
                if step in (STEP_EXP, STEP_EXP + 2):
                    if step == STEP_EXP:
                        pe_.wait_ge(low_done, 1)
                        pe_.wait_ge(wt_evac, 1)
                        pe_.wait_ge(exp_done, NG)
                    up((step - STEP_EXP) // 2)

            def down(u):
                h, e = divmod(u, E)
                pe_.wait_ge(lo_done[u % 2], u + 2 - u % 2)
                wait(pe_, w2_lo, min(u, E - 1) + 1)
                y = ps[:, 4 + h, :]
                cols = slice(2 * D, 3 * D)
                pe_.matmul(y, wh[:, e, cols], hh[:, u % HRING, :], start=False, stop=False, skip_group_check=True)
                pe_.matmul(y, wh[:, e, cols], hl[:, u % HRING, :], start=False, stop=False, skip_group_check=True)
                pe_.matmul(y, wl[:, e, cols], hh[:, u % HRING, :], start=False, stop=True,
                           skip_group_check=True).then_inc(w2_done, 1)

            def open_sum(h):
                pe_.wait_ge(wt_evac, h + 1)
                pe_.matmul(ps[:, 4 + h, :], b2_twice[:, :], wt_t[:, half(h)], start=True, stop=True).then_inc(b2_mm, 1)

            def y_back(k):
                pe_.wait_ge(y_evac, k + 1)
                for i, b in enumerate(SETS[k]):
                    t = pe_.transpose(ps[:, stage_bank("experts", k), tok(i)], y_t[:, tok(b)], ident)
                t.then_inc(y_tr, 1)

            def queries(k):
                pe_.wait_ge(xn_t_ready, HALVES + norm_count(3, k))
                pe_.matmul(ps[:, stage_bank("queries", k), set_cols(k)], wb[:, W_Q1:W_Q1 + D], xn_t[:, set_tok(k)],
                           start=True, stop=True).then_inc(q1_mm, 1)

            def scores(k):
                pe_.wait_ge(q1_evac, k + 1)
                for i, b in enumerate(SETS[k]):
                    m = pe_.matmul(ps[:, stage_bank("scores", k), tok(i)], q1_t[:, tok(b)], k1_t[:, tok(b)],
                                   start=True, stop=True)
                m.then_inc(s1_mm, 1)

            def turn_probabilities(k):
                pe_.wait_ge(p_done, k + 1)
                for i, b in enumerate(SETS[k]):
                    t = pe_.transpose(ps[:, stage_bank("probabilities", k), tok(i)], pr[:, b, :], ident)
                t.then_inc(p_tr, 1)

            def by_values(k):
                pe_.wait_ge(p_evac, k + 1)
                for i, b in enumerate(SETS[k]):
                    m = pe_.matmul(ps[:, stage_bank("values", k), tok(i)], pr_t[:, b, :], v1[:, b, :],
                                   start=True, stop=True)
                m.then_inc(av1_mm, 1)

            def last_product(k):
                pe_.wait_ge(xn_t_ready, HALVES + norm_count(4, k))
                for i, b in enumerate(SETS[k]):
                    m = pe_.matmul(ps[:, stage_bank("last", k), tok(i)], xn_t[:, tok(b)], wf[:, 1, :],
                                   start=True, stop=True)
                m.then_inc(f_mm, 1)

            pe_.wait_ge(o_done, B)
            pe_.wait_ge(b2_ready, 1)
            open_sum(0)
            for u in range(EARLY, 2 * E):
                if u == E:
                    pe_.wait_ge(low_done, 2)
                up(u)
                if u >= HRING:
                    down(u - HRING)
                if u == 4:
                    pe_.wait_ge(x1_done, B)
                    norm_turn(2, 1)
                if u == 6:
                    gate_scores(1)
                if u == 12:
                    turn_weights(1)
                if u == 14:
                    open_sum(1)
                if u == E + 5:
                    y_back(0)
                if u == E + 9:
                    norm_turn(3, 0)
                if u == E + 11:
                    queries(0)
                if u == E + 13:
                    scores(0)
            turn_probabilities(0)
            for u in range(2 * E - HRING, 2 * E):
                if u == 2 * E - 2:
                    by_values(0)
                down(u)
            late = (1, 2)
            for k in late:
                y_back(k)
            norm_turn(4, 0)
            for k in late:
                norm_turn(3, k)
            for k in late:
                queries(k)
            last_product(0)
            for k in late:
                scores(k)
            for k in late:
                turn_probabilities(k)
            for k in late:
                by_values(k)
            for k in late:
                norm_turn(4, k)
            for k in late:
                last_product(k)

        @block.vector
        def _(dve):
            chain = [0]

            def link(ins):
                chain[0] += 1
                ins.then_inc(vec, 1)
                dve.wait_ge(vec, chain[0])

            def statistics(src, bs):
                for b in bs:
                    s = dve.bn_stats(stats[:, b, :], src[:, b, :])
                link(s)
                for b in bs:
                    s = dve.bn_aggr(mv[:, b, :], stats[:, b, :])
                link(s)
                dve.tensor_scalar(var_eps[:, bs.start:bs.stop], mv[:, bs.start:bs.stop, 1:2]
                                  .rearrange("p b o -> p (b o)"), EPS, None, ALU.add).then_inc(var_ready, 1)

            def scaled(src, bs):
                for b in bs:
                    s = dve.tensor_scalar(xn[:, b, :], src[:, b, :], mv[:, b, 0:1], rstd[:, b:b + 1], ALU.subtract,
                                          ALU.mult)
                return s

            def normalise(norm, k, src):
                dve.wait_ge(rstd_ready, 1 + norm_count(norm, k))
                scaled(src, norm_range(norm, k)).then_inc(xn_ready, 1)

            def norm_low(h):
                dve.wait_ge(xn_t_ready, HALVES + norm_count(2, h))
                dve.tensor_tensor(xl[:, half(h)], ps[:, norm_bank(2, h), :], xh[:, half(h)].bitcast(F32),
                                  ALU.subtract).then_inc(low_done, 1)

            def gate_out(h):
                dve.wait_ge(gate_mm, h + 1)
                dve.tensor_copy(raw[:, seqs(h), :], ps[:, gate_bank(h), 0:HB * E].rearrange("p (b e) -> p b e", b=HB))\
                    .then_inc(gate_evac, 1)

            def compare_groups(h):
                r, g = raw[:, seqs(h), :], gmax[:, seqs(h), :]
                dve.memset(cand[:, seqs(h), 0:4], BIG)
                dve.wait_ge(gate_evac, h + 1)
                link(dve.tensor_reduce(g.rearrange("p b g -> p (b g)"), r.rearrange("p b (g e) -> p (b g) e", g=G), AX,
                                       ALU.max))
                mine = g.unsqueeze(3).broadcast_to([P, HB, G, G])
                other = g.unsqueeze(2).broadcast_to([P, HB, G, G])
                dve.tensor_tensor(cmp_a[:, seqs(h)], other, mine, ALU.is_gt)
                link(dve.tensor_tensor(cmp_b[:, seqs(h)], other, mine, ALU.is_ge))

            def rank_groups(h):
                above, level, place = cmp_a[:, seqs(h)], cmp_b[:, seqs(h)], rank[:, seqs(h), :]
                before = wb[:, W_LOW:W_LOW + G * G].rearrange("p (g o) -> p g o", g=G).unsqueeze(1)\
                    .broadcast_to([P, HB, G, G])
                link(dve.tensor_tensor(level, level, before, ALU.mult))
                link(dve.tensor_tensor(above, above, level, ALU.max))
                link(dve.tensor_reduce(place, above, AX, ALU.add))

            def candidates(h):
                r, place = raw[:, seqs(h), :], rank[:, seqs(h), :]
                link(dve.tensor_scalar(place, place, 2.0, -BIG, ALU.is_ge, ALU.mult))
                link(dve.tensor_tensor(cand[:, seqs(h), 4:4 + E].rearrange("p b (g e) -> p b g e", g=G),
                                       r.rearrange("p b (g e) -> p b g e", g=G),
                                       place.unsqueeze(3).broadcast_to([P, HB, G, EG]), ALU.add))
                for b in seqs_range(h):
                    m = dve.max(top8[:, b, :], cand[:, b, :])
                link(m)

            def mark_chosen(h):
                for b in seqs_range(h):
                    m = dve.match_replace(left[:, b, :], top8[:, b, :], cand[:, b, :], TAKEN)
                link(m)

            def sigmoids(h):
                sig = sg[:, seqs(h)]
                dve.wait_ge(gate_exp, h + 1)
                link(dve.tensor_scalar(sig, sig, 1.0, None, ALU.add))
                link(dve.reciprocal(sig, sig))

            def share(h):
                sig, chosen, w, total = (t[:, seqs(h)] for t in (sg, left, wts, wsum))
                link(dve.scalar_tensor_tensor(w, chosen[:, :, 4:4 + E], (BIG + TAKEN) / 2, sig, ALU.is_ge, ALU.mult))
                link(dve.tensor_reduce(total, w, AX, ALU.add))
                link(dve.reciprocal(total, total))
                link(dve.tensor_scalar(total, total, ROUTE_SCALE / 2, None, ALU.mult))
                dve.tensor_tensor(w, w, total.unsqueeze(2).broadcast_to([P, HB, E]), ALU.mult).then_inc(wts_ready, 1)

            def weights_out(h):
                dve.wait_ge(wts_tr, h + 1)
                dve.tensor_copy(wt_t[:, half(h)], ps[0:E, wts_bank(h), :]).then_inc(wt_evac, 1)

            def low_h(u):
                w = u % HRING
                dve.wait_ge(hi_done, u + 1)
                dve.tensor_tensor(hl[:, w, :], hw[:, w, :], hh[:, w, :].bitcast(F32),
                                  ALU.subtract).then_inc(lo_done[u % 2], 2)

            def product(u):
                e, s = u % E, u % 2
                dve.wait_ge(act_t, u + 1)
                dve.scalar_tensor_tensor(uu[:, s, :], th[:, s, :], 1.0, a1[:, s, :], ALU.add,
                                         ALU.mult).then_inc(vec_u, 1)
                if u < E:
                    split2(e)
                dve.wait_ge(c_ready, u + 1)
                wait(dve, mult_done, u - 1)
                dve.wait_ge(vec_u, u + 1)
                dve.scalar_tensor_tensor(h0[:, s, :], ps[:, 2 + s, :], bcol[:, e, 2:3], uu[:, s, :], ALU.add,
                                         ALU.mult).then_inc(h0_done, 1)

            def split2(e):
                dve.wait_ge(w_hi, e + 1)
                dve.tensor_tensor(wl[:, bass.ds(e, 1), 2 * D:3 * D], w_of(e)[:, :, 2 * D:3 * D],
                                  wh[:, bass.ds(e, 1), 2 * D:3 * D].bitcast(F32), ALU.subtract).then_inc(w2_lo, 1)

            dve.wait_ge(x_in, 16)
            statistics(x0, range(B))
            dve.wait_ge(rstd_ready, 1)
            for h in range(HALVES):
                scaled(x0, seqs_range(h)).then_inc(xn_ready, 1)
            for n in range(4):
                col = A_COL + (1 - n % 2)
                dve.wait_ge(part1, n + 1)
                wait(dve, part2, n - 1)
                r = rest[:, n % 2, :]
                dve.scalar_tensor_tensor(r, ps[:, n, :], wa[:, col:col + 1], parts[n][:, 0, :], ALU.add,
                                         ALU.subtract).then_inc(rest_ready, 1)
                dve.wait_ge(part2, n + 1)
                dve.tensor_tensor(parts[n][:, 2, :], r, parts[n][:, 1, :], ALU.subtract).then_inc(part3, 1)
            dve.wait_ge(row_in, 16)
            dve.wait_ge(xn_tr, HALVES)
            for n in range(4):
                dve.wait_ge(v_proj, n + 1)
                bank = ps[:, 6 + n % 2, :].rearrange("p (i w) -> p i w", i=2)
                bv = row_sb[:, D:3 * D]
                two = slice(2 * n, 2 * n + 2)
                dve.tensor_tensor(xn[:, two, :], bank[:, :, 0:D], bv[:, 0:D].unsqueeze(1).broadcast_to([P, 2, D]),
                                  ALU.add)
                dve.tensor_tensor(v1[:, two, :], bank[:, :, D:2 * D],
                                  bv[:, D:2 * D].unsqueeze(1).broadcast_to([P, 2, D]), ALU.add).then_inc(v_evac, 1)
            dve.wait_ge(tg_ready, 1)
            dve.scalar_tensor_tensor(x0[:, :, :], row_sb[:, 0:D].unsqueeze(1).broadcast_to([P, B, D]), tg[:, 0:1],
                                     x0[:, :, :], ALU.mult, ALU.add).then_inc(xb_ready, 1)

            for step in range(STEPS):
                if step == STEP_N2:
                    dve.wait_ge(x1_done, HB)
                    statistics(x1, seqs_range(0))
                if step == STEP_N2 + 1:
                    normalise(2, 0, x1)
                if step == STEP_N2 + 3:
                    norm_low(0)
                if step == STEP_N2 + 4:
                    gate_out(0)
                if step == STEP_N2 + 5:
                    compare_groups(0)
                    rank_groups(0)
                if step == STEP_N2 + 6:
                    candidates(0)
                    mark_chosen(0)
                if step == STEP_N2 + 7:
                    sigmoids(0)
                    share(0)
                if step == STEP_N2 + 9:
                    weights_out(0)
                if step in (STEP_EXP + 1, STEP_EXP + 3):
                    u = (step - STEP_EXP - 1) // 2
                    product(u)
                j = step
                if j < NG:
                    b, g = divmod(j, GROUPS)
                    dve.wait_ge(s_ready, j + 1)
                    m = dve.tensor_reduce(negm[:, b % 2, g * GH:(g + 1) * GH],
                                          ps[:, j % 2, :].rearrange("p (i k) -> p i k", i=GH), AX, ALU.max,
                                          negate=True)
                    m.then_inc(max_done, 1)
                    if g == GROUPS - 1:
                        dve.wait_ge(max_done, j + 1)
                        wait(dve, t_ready, t_before_negm(b - 2) + 1 if b >= 2 else 0)
                        link(dve.tensor_copy(negm_parts[:, b % 2, 0:H], negm[:, b % 2, :]))
                        dve.tensor_tensor(negm_parts[:, b % 2, H:2 * H], negm[:, b % 2, :], negm_parts[:, b % 2, 0:H],
                                          ALU.subtract).then_inc(negm_ready, 1)
                j = step - ST_LAG - 1
                if 0 <= j < NG and by_vec(j):
                    dve.wait_ge(exp_done, j + 1)
                    wait(dve, av_done, j - RING + 1)
                    dve.tensor_tensor(p2[:, j % RING, :], pe[:, j % RING, :], p1[:, j % RING, :],
                                      ALU.subtract).then_inc(p2_vec, 1)
                if step % GROUPS == 0:
                    b = step // GROUPS - 4
                    if 0 <= b < B:
                        dve.wait_ge(av_done, GROUPS * (b + 1))
                        wait(dve, t_ready, t_before_o(b - 2) + 1 if b >= 2 else 0)
                        o = ps[:, 4 + b % 2, 0:H * VC].rearrange("p (h v) -> p h v", h=H)
                        dve.tensor_reduce(o_sum[:, b % 2, :].rearrange("p (h d) -> p h d", h=H),
                                          o[:, :, 0:3 * HD].rearrange("p h (t d) -> p h d t", t=3), AX, ALU.add)
                        link(dve.reciprocal(den[:, b % 2, :], o[:, :, 3 * HD:VC].rearrange("p h v -> p (h v)")))
                        dve.tensor_tensor(o_nat[:, b % 2, :].rearrange("p (h d) -> p h d", h=H),
                                          o_sum[:, b % 2, :].rearrange("p (h d) -> p h d", h=H),
                                          den[:, b % 2, :].unsqueeze(2).broadcast_to([P, H, HD]),
                                          ALU.mult).then_inc(o_done, 1)
                if step % GROUPS == 3:
                    b = step // GROUPS - 4
                    if 0 <= b < B:
                        dve.wait_ge(o_proj, b + 1)
                        dve.wait_ge(xb_ready, 1)
                        dve.scalar_tensor_tensor(x1[:, b, :], ps[:, 7, 0:D], tg[:, 0:1], x0[:, b, :], ALU.mult,
                                                 ALU.add).then_inc(x1_done, 1)

            def after_experts(k):
                dve.wait_ge(y_tr, k + 1)
                link(dve.scalar_tensor_tensor(flat(x2[:, set_seqs(k), :]), ps[:, stage_bank("experts", k), set_cols(k)],
                                              tg[:, 2:3], flat(x1[:, set_seqs(k), :]), ALU.mult, ALU.add))
                statistics(x2, SETS[k])

            def maxima(k):
                dve.wait_ge(s1_mm, k + 1)
                link(dve.tensor_reduce(negm1[:, 0, set_seqs(k)],
                                       ps[:, stage_bank("scores", k), set_cols(k)].rearrange("p (b k) -> p b k", k=P),
                                       AX, ALU.max, negate=True))
                dve.tensor_scalar(negm1[:, 1, set_seqs(k)], negm1[:, 0, set_seqs(k)], scale1, None,
                                  ALU.mult).then_inc(negm1_done, 1)

            def probabilities_out(k):
                dve.wait_ge(p_tr, k + 1)
                dve.tensor_copy(flat(pr_t[:, set_seqs(k), :]),
                                ps[:, stage_bank("probabilities", k), set_cols(k)]).then_inc(p_evac, 1)
                link(dve.reciprocal(den1[:, 1, set_seqs(k)], den1[:, 0, set_seqs(k)]))
                link(dve.tensor_scalar(den1[:, 1, set_seqs(k)], den1[:, 1, set_seqs(k)], tg[:, 1:2], None, ALU.mult))

            def after_attention(k):
                dve.wait_ge(av1_mm, k + 1)
                for i, b in enumerate(SETS[k]):
                    m = dve.scalar_tensor_tensor(x3[:, b, :], ps[:, stage_bank("values", k), tok(i)],
                                                 den1[:, 1, b:b + 1], x2[:, b, :], ALU.mult, ALU.add)
                link(m)
                statistics(x3, SETS[k])

            def last_bias(k):
                dve.wait_ge(f_mm, k + 1)
                dve.tensor_tensor(ff[:, set_seqs(k), :],
                                  ps[:, stage_bank("last", k), set_cols(k)].rearrange("p (b d) -> p b d", d=D),
                                  row_sb[:, 3 * D:4 * D].unsqueeze(1).broadcast_to([P, len(SETS[k]), D]),
                                  ALU.add).then_inc(f_add, 1)

            def result(k):
                dve.wait_ge(f_tanh, k + 1)
                dve.scalar_tensor_tensor(x4[:, set_seqs(k), :], fft[:, set_seqs(k), :], tg[:, 3:4],
                                         x3[:, set_seqs(k), :], ALU.mult, ALU.add).then_inc(x4_done, 1)

            dve.wait_ge(x1_done, B)
            statistics(x1, seqs_range(1))
            for u in range(EARLY, 2 * E):
                if u >= 3 and u % 2:
                    low_h(u - 3)
                product(u)
                if u == 2:
                    normalise(2, 1, x1)
                if u == 5:
                    norm_low(1)
                if u == 6:
                    gate_out(1)
                    compare_groups(1)
                if u == 7:
                    rank_groups(1)
                if u == 8:
                    candidates(1)
                if u == 9:
                    mark_chosen(1)
                    sigmoids(1)
                if u == 10:
                    share(1)
                if u == 13:
                    weights_out(1)
                if u == E + 5:
                    after_experts(0)
                if u == E + 7:
                    normalise(3, 0, x2)
                if u == E + 13:
                    maxima(0)
            probabilities_out(0)
            dve.wait_ge(lo_done[1], 2 * E - 4)
            low_h(2 * E - 3)
            low_h(2 * E - 2)
            low_h(2 * E - 1)
            after_attention(0)
            late = (1, 2)
            after_experts(1)
            normalise(4, 0, x3)
            after_experts(2)
            for k in late:
                normalise(3, k, x2)
            last_bias(0)
            for k in late:
                maxima(k)
            result(0)
            for k in late:
                probabilities_out(k)
            for k in late:
                after_attention(k)
            for k in late:
                normalise(4, k, x3)
            for k in late:
                last_bias(k)
            for k in late:
                result(k)


def kernel(**inputs):
    import concourse.bacc as bacc
    from concourse.bass_utils import run_bass_kernel_spmd

    v = {name: np.asarray(a) for name, a in inputs.items()}

    def by_depth(a):
        return a.reshape(H, HD, -1).transpose(1, 0, 2).reshape(D, -1)

    low = np.tril(np.ones((G, G), np.float32), -1).reshape(1, G * G)
    arrays = {
        "x": v["x"],
        "ctx_t": v["ctx_1024"].reshape(T, D).T,
        "w_a": np.concatenate([
            by_depth(v["L0_xattn_wk"]).T, by_depth(v["L0_xattn_wq"]).T, np.eye(P, dtype=np.float32),
            by_depth(v["L0_xattn_bq"]), by_depth(v["L0_xattn_bk"]),
            v["L1_xattn_bq"][:, None], v["L1_xattn_bk"][:, None]], axis=1),
        "w_b": np.concatenate([
            v["L0_xattn_wv"].T, v["L1_xattn_Wv"], v["L0_xattn_wo"].T, v["L1_xattn_Wq"], v["L1_xattn_Wk"],
            v["L1_ffn_weight"].T, v["L1_ffn_aux_weight1"].T, v["L1_ffn_aux_weight2"], v["L0_ffn_Wg"].T,
            np.repeat(low, P, axis=0)], axis=1),
        "rows": np.concatenate([v["L0_xattn_bo"], v["L0_xattn_bv"], v["L1_xattn_bv"], v["L1_ffn_bias"]])[None],
        "gates": np.concatenate([v["g_xattn"], v["g_ffn"]])[None],
        "b2": v["L0_ffn_b2"],
        "w_big": np.concatenate([v[n].transpose(2, 0, 1) for n in ("L0_ffn_W1", "L0_ffn_W3", "L0_ffn_W2")], axis=2),
        "b_cols": np.stack([v["L0_ffn_b1"].T, v["L0_ffn_b3"].T], axis=2),
    }
    nc = bacc.Bacc("TRN2", target_bir_lowering=False, num_devices=1)
    args = []
    for name in arrays:
        arrays[name] = np.ascontiguousarray(arrays[name])
        args.append(nc.dram_tensor(name, arrays[name].shape, F32, kind="ExternalInput").ap())
    args.append(nc.dram_tensor("out", (B, P, D), F32, kind="ExternalOutput").ap())
    flamingo(nc, *args)
    done = run_bass_kernel_spmd(nc, [arrays], core_ids=[0])
    return done.results[0]["out"]
```

```python
import numpy as np

import concourse.bass as bass
from concourse import mybir
from contextlib import ExitStack

F32 = mybir.dt.float32
F32R = mybir.dt.float32r
BF16 = mybir.dt.bfloat16
F16 = mybir.dt.float16
U32 = mybir.dt.uint32
ALU = mybir.AluOpType
ACT = mybir.ActivationFunctionType
AX = mybir.AxisListType.X

P = 128
D = 128
B = 8
HALVES = 2
HB = B // HALVES
HT = HB * P
T = B * P
H = 16
HD = D // H
E = 16
G = 4
EG = E // G
EPS = 1e-5
ROUTE_SCALE = 2.5
BIG = 3.0e38
TAKEN = 3.3e38

A_WK, A_WQ, A_ID, A_COL = 0, D, 2 * D, 3 * D
A_W = 3 * D + 4
(W_V, W_O, W_Q1, W_K1, W_F, W_A1, W_A2, W_G, W_LOW) = (0, 256, 384, 512, 640, 768, 896, 1024, 1024 + E)
B_W = W_LOW + G * G

Q_PARTS = (0, 0, 0, 1, 1, 2)
K_PARTS = (0, 1, 2, 0, 1, 0)
MAX_ROW = HD * len(Q_PARTS)

TWO_ONES = 0x3F803F80

GROUPS = 4
GH = H // GROUPS
NG = B * GROUPS
ST_LAG = 9
AV_LAG = ST_LAG + 3
VC = 3 * HD + 1
RING = 4
SETS = (range(0, HB), range(HB, HB + 2), range(HB + 2, B))
STEPS = NG + AV_LAG + GROUPS + 1
EARLY = 4
CHUNKS = ((0, 4), (4, 7), (7, 10), (10, 14), (14, 16))
STARTED = 2
AHEAD = 6
HIGH_STEPS = (20, 24, 28, 32, 36, 40)
LOW2_STEPS = (35, 36, 37, 38, 39, 42)
LOW_GROUPS = (15, 19, 24, 28)
STEP_N2 = 32
STEP_EXP = 43
HRING = 6
DOWN_LAG = 5
WEB = 4


def flamingo(nc, x, ctx_t, w_a, w_b, rows, gates, b2, w_big, b_cols, out):
    scale0 = float(HD) ** -0.5
    scale1 = float(D) ** -0.5
    web_dram = nc.dram_tensor("web_dram", [E, T], F32, kind="Internal").ap()

    stack = ExitStack()
    with stack:
        def sb(name, shape, dt=F32):
            return stack.enter_context(nc.sbuf_tensor(name, shape, dt))

        def sem(name):
            return stack.enter_context(nc.semaphore(name))

        def set_seqs(k):
            return slice(SETS[k].start, SETS[k].stop)

        def set_tok(k):
            return slice(SETS[k].start * P, SETS[k].stop * P)

        def set_cols(k):
            return slice(0, len(SETS[k]) * P)

        def norm_range(norm, k):
            return seqs_range(k) if norm <= 2 else SETS[k]

        def flat(ap):
            return ap.rearrange("p b t -> p (b t)")

        x0 = sb("x0", [P, B, D])
        x1 = sb("x1", [P, B, D])
        x2 = x0
        x3 = x1
        xn = sb("xn", [P, B, D])
        xn_t = sb("xn_t", [P, T])
        xl = sb("xl", [P, T], F32R)
        w_first = sb("w_first", [P, EARLY, 3 * D])
        ctx_sb = flat(w_first[:, :, :])[:, 0:T]
        wa = sb("wa", [P, A_W])
        wb = sb("wb", [P, B_W])
        row_sb = sb("row_sb", [P, 4 * D])
        ones_row = sb("ones_row", [1, P])
        gate_sb = sb("gate_sb", [P, 4])
        tg = sb("tg", [P, 4])
        b2_sb = sb("b2_sb", [E, D])
        b2_twice = sb("b2_twice", [E, D])
        wh = sb("wh", [P, E, 3 * D], F32R)
        wl = sb("wl", [P, E, 3 * D], F32R)
        bcol = sb("bcol", [P, E, 3])
        stats = sb("stats", [P, B, 6])
        mv = sb("mv", [P, B, 2])
        var_eps = sb("var_eps", [P, B])
        rstd = sb("rstd", [P, B])
        minus_half = sb("minus_half", [P, B])
        identb = sb("identb", [P, P], BF16)
        rest = x1[:, :, :].rearrange("p b d -> p (b d)").rearrange("p (s t) -> p s t", s=2)
        qs = sb("qs", [P, HALVES, H, HT], BF16)
        ks = sb("ks", [P, HALVES, H, HT], BF16)
        v_parts = sb("v_parts", [P, B * H, VC], BF16)
        values = sb("values", [P, 2, B, D])
        v0_flat, v1 = flat(values[:, 0, :, :]), values[:, 1, :, :]
        k1_t = sb("k1_t", [P, T])
        negm = sb("negm", [P, 2, H])
        negm_parts = sb("negm_parts", [P, 2, 2 * H], BF16)
        negm_rows = sb("negm_rows", [2 * H, 2, P], BF16)
        o_sum = sb("o_sum", [P, 2, D])
        o_nat = sb("o_nat", [P, 2, D])
        o_t = sb("o_t", [P, 2, P])
        den = sb("den", [P, 2, H])
        wf = sb("wf", [P, 2, D])
        raw = sb("raw", [P, B, E])
        sg = sb("sg", [P, B, E])
        gmax = sb("gmax", [P, B, G])
        cmp_a = sb("cmp_a", [P, B, G, G])
        cmp_b = sb("cmp_b", [P, B, G, G])
        rank = sb("rank", [P, B, G])
        cand = sb("cand", [P, B, 4 + E])
        top8 = sb("top8", [P, B, 8])
        left = sb("left", [P, B, 4 + E])
        wts = sb("wts", [P, B, E])
        wsum = sb("wsum", [P, B])
        wt_t = v0_flat[0:E, :]
        with ExitStack() as first:
            def once(name, shape, dt=F32):
                return first.enter_context(nc.sbuf_tensor(name, shape, dt))

            pe = once("pe", [P, RING, GH * P])
            p1 = once("p1", [P, RING, GH * P], F16)
            p2 = once("p2", [P, RING, GH * P], F16)
            parts = [once(f"parts{n}", [P, 3, HT], BF16) for n in range(4)]
        hh = sb("hh", [P, HRING, HT], F32R)
        hl = sb("hl", [P, HRING, HT], F32R)
        xh = sb("xh", [P, T], F32R)
        qs_free = qs[:, :, :, :].rearrange("p s h t -> p (s h t)").bitcast(F32)
        a1, th, uu = (qs_free[:, n * T:(n + 1) * T].rearrange("p (s t) -> p s t", s=2) for n in range(3))
        web = qs_free[:, 3 * T:3 * T + WEB * HT].rearrange("p (s t) -> p s t", s=WEB)
        hw = qs_free[:, 8 * T - HRING * HT:8 * T].rearrange("p (s t) -> p s t", s=HRING)
        ks_free = ks[:, :, :, :].rearrange("p s h t -> p (s h t)").bitcast(F32)
        y_t, q1_t, pr, pr_t, fft, x4 = (ks_free[:, n * T:(n + 1) * T] for n in range(6))
        pr, pr_t, fft, x4 = (t.rearrange("p (b t) -> p b t", b=B) for t in (pr, pr_t, fft, x4))
        w_rest = ks_free[:, 0:(E - EARLY) * 3 * D].rearrange("p (e w) -> p e w", e=E - EARLY)
        negm1 = sb("negm1", [P, 2, B])
        den1 = sb("den1", [P, 2, B])

        ps = stack.enter_context(nc.psum_tensor("ps", [P, 8, 512], F32))
        ident = wa[:, A_ID:A_ID + P]

        x_in, ctx_in = ([sem(f"{n}_in{h}") for h in range(HALVES)] for n in ("x", "ctx"))
        wa_in, wb_in, row_in, gate_in, b2_in, bcol_in = (
            sem(n) for n in ("wa_in", "wb_in", "row_in", "gate_in", "b2_in", "bcol_in"))
        rows_in = [sem(f"rows_in{n}") for n in range(4)]
        negm_in = [sem(f"negm_in{n}") for n in range(2)]
        web_in = [sem(f"web_in{n}") for n in range(WEB)]
        raw_in = [sem(f"raw_in{n}") for n in range(len(CHUNKS))]
        wt_out = sem("wt_out")
        out_done = sem("out_done")
        vec = sem("vec")
        vec_u = sem("vec_u")
        pads, pools_ready = sem("pads"), sem("pools_ready")
        var_ready, rstd_ready, xn_ready, xn_tr, xn_t_ready = (
            sem(n) for n in ("var_ready", "rstd_ready", "xn_ready", "xn_tr", "xn_t_ready"))
        proj_ready, part1, rest_ready, part2, part3 = (
            sem(n) for n in ("proj_ready", "part1", "rest_ready", "part2", "part3"))
        v_proj, v_evac, v_bias, v_part1, v_rest, v_part2, v_done = (
            sem(n) for n in ("v_proj", "v_evac", "v_bias", "v_part1", "v_rest", "v_part2", "v_done"))
        k1_proj, k1_evac, wf_mm, wf_evac, tg_ready, identb_ready, xb_ready, bcol_ready = (
            sem(n) for n in ("k1_proj", "k1_evac", "wf_mm", "wf_evac", "tg_ready", "identb_ready", "xb_ready",
                             "bcol_ready"))
        s_ready, max_done, negm_ready, t_ready, t_evac = (
            sem(n) for n in ("s_ready", "max_done", "negm_ready", "t_ready", "t_evac"))
        st_ready, exp_done, p2_pool, p2_vec, av_done = (
            sem(n) for n in ("st_ready", "exp_done", "p2_pool", "p2_vec", "av_done"))
        o_done, o_proj, x1_done = (sem(n) for n in ("o_done", "o_proj", "x1_done"))
        x_split, gate_mm, gate_evac, gate_exp, wts_ready, wts_tr, wt_evac, b2_ready, b2_mm, low_done = (
            sem(n) for n in ("x_split", "gate_mm", "gate_evac", "gate_exp", "wts_ready", "wts_tr", "wt_evac",
                             "b2_ready", "b2_mm", "low_done"))
        a_ready, c_ready, act_t, h0_done, mult_done, hi_done, w2_done = (
            sem(n) for n in ("a_ready", "c_ready", "act_t", "h0_done", "mult_done", "hi_done", "w2_done"))
        lo_done = [sem(f"lo_done{n}") for n in range(HRING)]
        w_hi, w13_lo, w2_lo = (sem(n) for n in ("w_hi", "w13_lo", "w2_lo"))
        y_evac, y_tr, q1_mm, q1_evac, s1_mm, negm1_done, p_done, p_tr, p_evac, av1_mm, f_mm, f_tanh, x4_done = (
            sem(n) for n in ("y_evac", "y_tr", "q1_mm", "q1_evac", "s1_mm", "negm1_done", "p_done", "p_tr", "p_evac",
                             "av1_mm", "f_mm", "f_tanh", "x4_done"))

        def wait(eng, s, count):
            if not isinstance(count, int) or count > 0:
                eng.wait_ge(s, count)

        def tok(b):
            return slice(b * P, (b + 1) * P)

        def half(h):
            return slice(h * HT, (h + 1) * HT)

        def seqs(h):
            return slice(h * HB, (h + 1) * HB)

        def seqs_range(h):
            return range(h * HB, (h + 1) * HB)

        def w_of(e):
            if e < EARLY:
                return w_first[:, e, :]
            return w_rest[:, e - EARLY, :]

        def wait_lo(eng, u):
            eng.wait_ge(lo_done[u % HRING], u // HRING + 1)

        def low_by_pool(u):
            return (u % 2 == 1 or u > E and u % 4 == 0) and u < 2 * E - 3

        def by_vec(j):
            return j % GROUPS == GROUPS - 1

        def wait_p2(eng, j):
            if j >= 0:
                if by_vec(j):
                    eng.wait_ge(p2_vec, j // GROUPS + 1)
                else:
                    eng.wait_ge(p2_pool, j - j // GROUPS + 1)

        def t_before_negm(b):
            return b + max(0, b - 3)

        def t_before_o(b):
            return min(B, b + 4) + b

        NORMS = [(1, 0), (1, 1), (2, 0), (2, 1), (3, 0), (3, 1), (3, 2), (4, 0), (4, 1), (4, 2)]

        def norm_count(norm, h):
            return NORMS.index((norm, h)) + 1

        def stage_bank(stage, k):
            n = ("experts", "norm 3", "queries", "scores", "probabilities", "values", "norm 4", "last").index(stage)
            return (6, 0, 2)[k] + n % 2

        def value_bank(n):
            return (6, 7, 4, 5)[n]

        def norm_bank(norm, h):
            return 4 + h if norm == 1 else (0, 6)[h] if norm == 2 else stage_bank(f"norm {norm}", h)

        def gate_bank(h):
            return (1, 7)[h]

        def wts_bank(h):
            return (0, 6)[h]

        block = stack.enter_context(nc.Block())

        @block.sync
        def _(sp):
            x_t = x.rearrange("b t d -> t b d")
            sp.dma_start(x0[:, seqs(0), :], x_t[:, seqs(0), :]).then_inc(x_in[0], 16)
            sp.dma_start(wa[:, :], w_a).then_inc(wa_in, 16)
            sp.dma_start(x0[:, seqs(1), :], x_t[:, seqs(1), :]).then_inc(x_in[1], 16)
            for h in range(HALVES):
                sp.dma_start(ctx_sb[:, half(h)], ctx_t[:, half(h)]).then_inc(ctx_in[h], 16)
            sp.dma_start(wb[:, :], w_b).then_inc(wb_in, 16)
            sp.dma_start(row_sb[:, :], rows.partition_broadcast(P)).then_inc(row_in, 16)
            sp.dma_start(gate_sb[:, :], gates.partition_broadcast(P)).then_inc(gate_in, 16)
            def place_rows(n, part):
                dst, terms = (qs, Q_PARTS) if n % 2 else (ks, K_PARTS)
                sp.wait_ge(pads, n + 1)
                sp.wait_ge((part1, part2, part3)[part], n + 1)
                for r, term in enumerate(terms):
                    if term == part:
                        sp.dma_start(dst[r * HD:(r + 1) * HD, n // 2, :, :], parts[n][:, part, :])\
                            .then_inc(rows_in[n], 16)

            def place_maxima(b):
                sp.wait_ge(t_evac, t_before_negm(b) + 1)
                sp.dma_start(qs[MAX_ROW:MAX_ROW + 2, b // HB, :, tok(b % HB)], negm_rows[:, b % 2, :]).then_inc(negm_in[b % 2], 16)

            for n in range(3):
                for part in range(3):
                    place_rows(n, part)
            place_rows(3, 0)
            place_maxima(0)
            place_rows(3, 1)
            place_rows(3, 2)
            place_maxima(1)
            sp.dma_start(b2_sb[:, :], b2).then_inc(b2_in, 16)
            sp.dma_start(bcol[:, :, 1:3], b_cols).then_inc(bcol_in, 16)

            def bring_weights(c):
                lo, hi = CHUNKS[c]
                dst = w_first[:, :, :] if c == 0 else w_rest[:, lo - EARLY:hi - EARLY, :]
                sp.dma_start(dst, w_big[:, lo:hi, :]).then_inc(raw_in[c], 16)

            sp.wait_ge(v_proj, 4)
            sp.wait_ge(k1_proj, 2)
            bring_weights(0)
            for b in range(2, B):
                place_maxima(b)
                if b >= 5:
                    sp.wait_ge(st_ready, NG // HALVES)
                    bring_weights(b - 4)
            def store_weights(h):
                sp.wait_ge(wt_evac, h + 1)
                sp.dma_start(web_dram[:, half(h)], wt_t[:, half(h)]).then_inc(wt_out, 16)
                sp.wait_ge(wt_out, 16 * (h + 1))

            def spread(u, e, s, h):
                wait(sp, mult_done, u - (WEB - 1))
                sp.dma_start(web[:, s, :], web_dram[bass.ds(e, 1), half(h)].partition_broadcast(P))\
                    .then_inc(web_in[s], 16)

            sp.wait_ge(st_ready, NG)
            bring_weights(4)
            store_weights(0)
            for s in range(WEB):
                spread(s, s, s, 0)
            with sp.Fori(WEB, E - WEB + 1, WEB) as e:
                for s in range(WEB):
                    spread(e + s, e + s, s, 0)
            store_weights(1)
            with sp.Fori(0, E - WEB + 1, WEB) as e:
                for s in range(WEB):
                    spread(e + (E + s), e + s, s, 1)
            out_t = out.rearrange("b t d -> t b d")
            for k in range(len(SETS)):
                sp.wait_ge(x4_done, k + 1)
                sp.dma_start(out_t[:, set_seqs(k), :], x4[:, set_seqs(k), :]).then_inc(out_done, 16)
            sp.wait_ge(out_done, 16 * len(SETS))

        @block.gpsimd
        def _(pool):
            def root(norm, k):
                bs = norm_range(norm, k)
                pool.wait_ge(var_ready, norm_count(norm, k))
                pool.tensor_tensor(rstd[:, bs.start:bs.stop], var_eps[:, bs.start:bs.stop],
                                   minus_half[:, bs.start:bs.stop], ALU.pow).then_inc(rstd_ready, 1)

            pool.memset(minus_half[:, :], -0.5).then_inc(pools_ready, 1)
            pool.memset(ones_row[:, :], 1.0).then_inc(pools_ready, 1)
            pool.memset(ks[:, 0, :, :].bitcast(U32), TWO_ONES).then_inc(pads, 1)
            pool.wait_ge(pools_ready, 2)
            for h in range(HALVES):
                root(1, h)
            pool.memset(qs[:, 0, :, :].bitcast(U32), 0).then_inc(pads, 1)
            pool.memset(ks[:, 1, :, :].bitcast(U32), TWO_ONES).then_inc(pads, 1)
            pool.memset(qs[:, 1, :, :].bitcast(U32), 0).then_inc(pads, 1)
            pool.memset(v_parts[:, :, VC - 1:VC], 1.0).then_inc(pools_ready, 1)
            def add_bias(w, h):
                pool.wait_ge(v_evac, 2 * h + 2)
                v, bias = values[:, w, seqs(h), :], row_sb[:, (w + 1) * D:(w + 2) * D]
                pool.tensor_tensor(v, v, bias.unsqueeze(1).broadcast_to([P, HB, D]), ALU.add).then_inc(v_bias, 1)

            pool.wait_ge(row_in, 16)
            def values_rest(h):
                hv = slice(h * HB * H, (h + 1) * HB * H)
                vf = v0_flat[:, half(h)].rearrange("p (n d) -> p n d", d=HD)
                pool.wait_ge(v_part1, h + 1)
                pool.tensor_tensor(vf, vf, v_parts[:, hv, 2 * HD:3 * HD], ALU.subtract).then_inc(v_rest, 1)

            def values_third(h):
                hv = slice(h * HB * H, (h + 1) * HB * H)
                vf = v0_flat[:, half(h)].rearrange("p (n d) -> p n d", d=HD)
                pool.wait_ge(v_part2, h + 1)
                pool.tensor_tensor(v_parts[:, hv, 0:HD], vf, v_parts[:, hv, HD:2 * HD],
                                   ALU.subtract).then_inc(v_done, 1)

            def split13(e):
                pool.wait_ge(w_hi, e + 1)
                pool.tensor_tensor(wl[:, e, 0:2 * D], w_of(e)[:, 0:2 * D],
                                   wh[:, e, 0:2 * D].bitcast(F32), ALU.subtract).then_inc(w13_lo, 1)

            add_bias(0, 0)
            values_rest(0)
            values_third(0)
            add_bias(0, 1)
            for j in range(NG):
                if j == 5:
                    values_rest(1)
                if j == 7:
                    values_third(1)
                if j in (10, 13):
                    add_bias(1, (j - 10) // 3)
                if j == STEP_N2 - ST_LAG:
                    root(2, 0)
                if j in LOW_GROUPS:
                    split13(LOW_GROUPS.index(j))
                if not by_vec(j):
                    pool.wait_ge(exp_done, j + 1)
                    wait(pool, av_done, j - RING + 1)
                    pool.tensor_tensor(p2[:, j % RING, :], pe[:, j % RING, :], p1[:, j % RING, :],
                                       ALU.subtract).then_inc(p2_pool, 1)

            def weight(u):
                w = u % HRING
                pool.wait_ge(web_in[u % WEB], (u // WEB + 1) * 16)
                pool.wait_ge(h0_done, u + 1)
                pool.tensor_tensor(hw[:, w, :], hw[:, w, :], web[:, u % WEB, :], ALU.mult).then_inc(mult_done, 1)

            def low_h(u):
                w = u % HRING
                pool.wait_ge(hi_done, u + 1)
                pool.tensor_tensor(hl[:, w, :], hw[:, w, :], hh[:, w, :].bitcast(F32),
                                   ALU.subtract).then_inc(lo_done[w], 1)

            for e in range(len(LOW_GROUPS), AHEAD):
                split13(e)
            for u in range(2 * E):
                if u + AHEAD < E:
                    split13(u + AHEAD)
                if u >= 3 and low_by_pool(u - 3):
                    low_h(u - 3)
                weight(u)
                if u == 1:
                    root(2, 1)
                if u == E + 6:
                    root(3, 0)
            for norm, k in NORMS[NORMS.index((3, 1)):]:
                root(norm, k)

        @block.scalar
        def _(act):
            act.wait_ge(pools_ready, 1)
            act.activation(identb[:, 0:1], minus_half[:, 0:1], ACT.Exp)
            act.wait_ge(wa_in, 16)
            def first_part(n):
                col = A_COL + (1 - n % 2)
                act.wait_ge(proj_ready, n + 1)
                act.activation(parts[n][:, 0, :], ps[:, n, :], ACT.Identity, bias=wa[:, col:col + 1]).then_inc(part1, 1)

            def second_part(n):
                act.wait_ge(rest_ready, n + 1)
                act.activation(parts[n][:, 1, :], rest[:, n % 2, :], ACT.Copy).then_inc(part2, 1)

            for h in range(HALVES):
                first_part(2 * h)
                act.wait_ge(xn_tr, h + 1)
                act.activation(xn_t[:, half(h)], ps[:, 4 + h, :], ACT.Copy).then_inc(xn_t_ready, 1)
                second_part(2 * h)
                first_part(2 * h + 1)
                second_part(2 * h + 1)
            act.activation(identb[:, :], ident, ACT.Copy).then_inc(identb_ready, 1)
            act.wait_ge(gate_in, 16)
            act.activation(tg[:, :], gate_sb[:, :], ACT.Tanh).then_inc(tg_ready, 1)
            def values_out(n):
                act.wait_ge(v_proj, n + 1)
                act.activation(values[:, :, 2 * n:2 * n + 2, :],
                               ps[:, value_bank(n), :].rearrange("p (i w d) -> p w i d", i=2, w=2),
                               ACT.Copy).then_inc(v_evac, 1)

            def values_part(n, h):
                hv = slice(h * HB * H, (h + 1) * HB * H)
                act.wait_ge((v_bias, v_rest)[n], h + 1)
                act.activation(v_parts[:, hv, (2 - n) * HD:(3 - n) * HD],
                               v0_flat[:, half(h)].rearrange("p (n d) -> p n d", d=HD),
                               ACT.Copy).then_inc((v_part1, v_part2)[n], 1)

            values_out(0)
            values_out(1)
            for h in range(HALVES):
                act.wait_ge(k1_proj, h + 1)
                act.activation(k1_t[:, half(h)], ps[:, 4 + h, :], ACT.Identity,
                               bias=wa[:, A_COL + 3:A_COL + 4]).then_inc(k1_evac, 1)

            def norm_out(norm, k):
                bs = norm_range(norm, k)
                columns, src = slice(bs.start * P, bs.stop * P), ps[:, norm_bank(norm, k), 0:len(bs) * P]
                act.wait_ge(xn_tr, norm_count(norm, k))
                if norm == 2:
                    act.activation(xh[:, columns], src, ACT.Copy)
                act.activation(xn_t[:, columns], src, ACT.Copy).then_inc(xn_t_ready, 1)

            def gate_exponential(h):
                act.wait_ge(gate_evac, h + 1)
                act.activation(sg[:, seqs(h), :], raw[:, seqs(h), :], ACT.Exp, scale=-1.0).then_inc(gate_exp, 1)

            def high_w(e):
                if isinstance(e, int):
                    act.wait_ge(raw_in[[e < hi for lo, hi in CHUNKS].index(True)], 16)
                act.activation(wh[:, e, :], w_of(e), ACT.Copy).then_inc(w_hi, 1)

            def high_h(u):
                w = u % HRING
                act.wait_ge(mult_done, u + 1)
                wait(act, w2_done, u - (HRING - 1))
                act.activation(hh[:, w, :], hw[:, w, :], ACT.Copy).then_inc(hi_done, 1)

            def first_product(u, e, s):
                act.wait_ge(a_ready, u + 1)
                wait(act, h0_done, u - 1)
                act.activation(a1[:, s, :], ps[:, s, :], ACT.Identity,
                               bias=bcol[:, e, 1:2])
                act.activation(th[:, s, :], ps[:, s, :], ACT.Tanh, scale=0.5,
                               bias=bcol[:, e, 0:1]).then_inc(act_t, 1)

            for step in range(STEPS):
                if step == 1:
                    act.wait_ge(pools_ready, 3)
                    values_part(0, 0)
                if step == 3:
                    values_part(1, 0)
                if step in (6, 7):
                    values_out(step - 4)
                if step == 14:
                    values_part(0, 1)
                if step == 16:
                    values_part(1, 1)
                if step in (8, 9):
                    n = step - 8
                    act.wait_ge(wf_mm, n + 1)
                    act.activation(wf[:, n, :], ps[:, 7, 0:D], ACT.Copy).then_inc(wf_evac, 1)
                if step == 16:
                    act.wait_ge(bcol_in, 16)
                    act.activation(bcol[:, :, 0:1], bcol[:, :, 1:2], ACT.Copy, scale=0.5).then_inc(bcol_ready, 1)
                    act.wait_ge(b2_in, 16)
                    act.activation(b2_twice[:, :], b2_sb[:, :], ACT.Copy, scale=2.0).then_inc(b2_ready, 1)
                if step == STEP_N2 + 5:
                    norm_out(2, 0)
                if step == STEP_N2 + 6:
                    gate_exponential(0)
                if step in HIGH_STEPS:
                    high_w(HIGH_STEPS.index(step))
                j = step - ST_LAG
                if 0 <= j < NG:
                    act.wait_ge(st_ready, j + 1)
                    wait_p2(act, j - RING)
                    act.activation(pe[:, j % RING, :], ps[:, 2 + j % 2, :], ACT.Exp, scale=scale0)
                    wait(act, av_done, j - RING + 1)
                    act.activation(p1[:, j % RING, :], ps[:, 2 + j % 2, :], ACT.Exp, scale=scale0).then_inc(exp_done, 1)
                if step % GROUPS == 1:
                    b = step // GROUPS - 1
                    if 0 <= b < B:
                        act.wait_ge(t_ready, t_before_negm(b) + 1)
                        if b >= 2:
                            act.wait_ge(negm_in[b % 2], 16 * (b // 2))
                        act.activation(negm_rows[:, b % 2, :], ps[0:2 * H, 6, 0:P // 2].bitcast(BF16),
                                       ACT.Copy).then_inc(t_evac, 1)
                if step % GROUPS == 2:
                    b = step // GROUPS - 4
                    if 0 <= b < B:
                        act.wait_ge(t_ready, t_before_o(b) + 1)
                        wait(act, o_proj, b - 1)
                        act.activation(o_t[:, b % 2, :], ps[:, 6, 0:P], ACT.Copy).then_inc(t_evac, 1)
                if step in (STEP_EXP + 1, STEP_EXP + 3):
                    u = (step - STEP_EXP - 1) // 2
                    first_product(u, u, u)
                    high_w(u + AHEAD)
            def y_out(k):
                h, first = divmod(SETS[k].start, HB)
                act.wait_ge(w2_done, E * (h + 1))
                act.activation(y_t[:, set_tok(k)], ps[:, 4 + h, first * P:(first + len(SETS[k])) * P],
                               ACT.Copy).then_inc(y_evac, 1)

            def queries(k):
                act.wait_ge(q1_mm, k + 1)
                act.activation(q1_t[:, set_tok(k)], ps[:, stage_bank("queries", k), set_cols(k)], ACT.Identity,
                               bias=wa[:, A_COL + 2:A_COL + 3]).then_inc(q1_evac, 1)

            def exponentials(k):
                act.wait_ge(negm1_done, k + 1)
                for i, b in enumerate(SETS[k]):
                    e = act.activation(pr[:, b, :], ps[:, stage_bank("scores", k), tok(i)], ACT.Exp, scale=scale1,
                                       bias=negm1[:, 1, b:b + 1], accum_out=den1[:, 0, b:b + 1])
                e.then_inc(p_done, 1)

            def last_tanh(k):
                act.wait_ge(f_mm, k + 1)
                act.activation(flat(fft[:, set_seqs(k), :]), ps[:, stage_bank("last", k), set_cols(k)],
                               ACT.Tanh).then_inc(f_tanh, 1)

            for u in range(STARTED, 2 * E):
                if u >= 3:
                    high_h(u - 3)
                first_product(u, u % E, u % 2)
                if u + AHEAD < E:
                    high_w(u + AHEAD)
                if u == 4:
                    norm_out(2, 1)
                if u == 7:
                    gate_exponential(1)
                if u == E + 4:
                    y_out(0)
                if u == E + 9:
                    norm_out(3, 0)
                if u == E + 11:
                    queries(0)
                if u == E + 14:
                    exponentials(0)
            for u in range(2 * E - 3, 2 * E):
                high_h(u)
            late = (1, 2)
            for k in late:
                y_out(k)
            for k in late:
                norm_out(3, k)
            for k in late:
                queries(k)
            for k in late:
                exponentials(k)
            norm_out(4, 0)
            last_tanh(0)
            for k in late:
                norm_out(4, k)
            for k in late:
                last_tanh(k)

        @block.tensor
        def _(pe_):
            def norm_turn(norm, k):
                pe_.wait_ge(xn_ready, norm_count(norm, k))
                turn_sequences(norm_range(norm, k), norm_bank(norm, k))

            def gate_scores(h):
                pe_.wait_ge(xn_t_ready, norm_count(2, h))
                for i in range(HB):
                    m = pe_.matmul(ps[:, gate_bank(h), i * E:(i + 1) * E], xn_t[:, tok(h * HB + i)],
                                   wb[:, W_G:W_G + E], start=True, stop=True)
                m.then_inc(gate_mm, 1)

            def turn_weights(h):
                pe_.wait_ge(wts_ready, h + 1)
                pe_.wait_ge(low_done, h + 1)
                for i in range(HB):
                    t = pe_.transpose(ps[0:E, wts_bank(h), tok(i)], wts[:, h * HB + i, :], ident)
                t.then_inc(wts_tr, 1)

            def turn_sequences(bs, bank):
                for i, b in enumerate(bs):
                    t = pe_.transpose(ps[:, bank, tok(i)], xn[:, b, :], ident)
                t.then_inc(xn_tr, 1)

            pe_.wait_ge(wa_in, 16)
            for h in range(HALVES):
                pe_.wait_ge(ctx_in[h], 16)
                pe_.matmul(ps[:, 2 * h, :], wa[:, A_WK:A_WK + D], ctx_sb[:, half(h)], start=True,
                           stop=True).then_inc(proj_ready, 1)
                pe_.wait_ge(xn_ready, h + 1)
                turn_sequences(seqs_range(h), 4 + h)
                pe_.wait_ge(xn_t_ready, h + 1)
                pe_.matmul(ps[:, 2 * h + 1, :], wa[:, A_WQ:A_WQ + D], xn_t[:, half(h)], start=True,
                           stop=True).then_inc(proj_ready, 1)
            def project_values(n):
                if n == 2:
                    pe_.wait_ge(k1_evac, 2)
                for i in range(2):
                    m = pe_.matmul(ps[:, value_bank(n), i * 2 * D:(i + 1) * 2 * D], ctx_sb[:, tok(2 * n + i)],
                                   wb[:, W_V:W_V + 2 * D], start=True, stop=True)
                m.then_inc(v_proj, 1)

            pe_.wait_ge(wb_in, 16)
            project_values(0)
            project_values(1)
            for h in range(HALVES):
                pe_.matmul(ps[:, 4 + h, :], wb[:, W_K1:W_K1 + D], ctx_sb[:, half(h)], start=True,
                           stop=True).then_inc(k1_proj, 1)

            def up(u):
                h, e = divmod(u, E)
                wait(pe_, w13_lo, min(u, E - 1) + 1)
                for bank, col, freed, ready in ((u % 2, 0, act_t, a_ready), (2 + u % 2, D, h0_done, c_ready)):
                    wait(pe_, freed, u - 1)
                    cols = slice(col, col + D)
                    pe_.matmul(ps[:, bank, :], wh[:, e, cols], xh[:, half(h)], start=True, stop=False)
                    pe_.matmul(ps[:, bank, :], wh[:, e, cols], xl[:, half(h)], start=False, stop=False)
                    pe_.matmul(ps[:, bank, :], wl[:, e, cols], xh[:, half(h)], start=False,
                               stop=True).then_inc(ready, 1)

            for step in range(STEPS):
                if step in (5, 6):
                    project_values(step - 3)
                if step == 7:
                    pe_.wait_ge(v_evac, 2)
                    pe_.matmul(ps[:, 7, 0:D], wb[:, W_A1:W_A1 + D], wb[:, W_A2:W_A2 + D], start=True,
                               stop=True).then_inc(wf_mm, 1)
                if step == 8:
                    pe_.wait_ge(wf_evac, 1)
                    pe_.matmul(ps[:, 7, 0:D], wb[:, W_F:W_F + D], wf[:, 0, :], start=True, stop=True).then_inc(wf_mm, 1)
                if step == STEP_N2 + 5:
                    pe_.wait_ge(max_done, NG)
                    norm_turn(2, 0)
                if step == STEP_N2 + 6:
                    gate_scores(0)
                if step == STEP_N2 + 9:
                    turn_weights(0)
                j = step
                if j < NG:
                    b, g = divmod(j, GROUPS)
                    if j % (GROUPS * HB) == 0:
                        for n in (0, 1):
                            pe_.wait_ge(rows_in[2 * (b // HB) + n], 16 * len(Q_PARTS))
                    if j == 0:
                        pe_.wait_ge(rest_ready, 2)
                    wait(pe_, max_done, j - 1)
                    for i in range(GH):
                        q, k = (t[:, b // HB, g * GH + i, tok(b % HB)] for t in (qs, ks))
                        m = pe_.matmul(ps[:, j % 2, tok(i)], q, k, start=True, stop=True)
                    m.then_inc(s_ready, 1)
                j = step - ST_LAG
                if j == 0:
                    pe_.wait_ge(rest_ready, 4)
                if 0 <= j < NG:
                    b, g = divmod(j, GROUPS)
                    if g == 0:
                        pe_.wait_ge(negm_in[b % 2], 16 * (b // 2 + 1))
                    wait(pe_, exp_done, j - 1)
                    for i in range(GH):
                        q, k = (t[:, b // HB, g * GH + i, tok(b % HB)] for t in (qs, ks))
                        m = pe_.matmul(ps[:, 2 + j % 2, tok(i)], k, q, start=True, stop=True)
                    m.then_inc(st_ready, 1)
                j = step - AV_LAG
                if 0 <= j < NG:
                    b, g = divmod(j, GROUPS)
                    if j == 0:
                        pe_.wait_ge(v_evac, 4)
                    if j % (GROUPS * HB) == 0:
                        pe_.wait_ge(v_done, b // HB + 1)
                    if g == 0:
                        wait(pe_, o_done, b - 1)
                    wait_p2(pe_, j)
                    for i in range(GH):
                        hd = g * GH + i
                        pe_.matmul(ps[:, 4 + b % 2, hd * VC:(hd + 1) * VC], p1[:, j % RING, tok(i)],
                                   v_parts[:, b * H + hd, :], start=True, stop=True)
                        m = pe_.matmul(ps[:, 4 + b % 2, hd * VC + HD:(hd + 1) * VC], p2[:, j % RING, tok(i)],
                                       v_parts[:, b * H + hd, HD:VC], start=False, stop=True, skip_group_check=True)
                    m.then_inc(av_done, 1)
                if step % GROUPS == 1:
                    b = step // GROUPS - 1
                    if 0 <= b < B:
                        if b == 0:
                            pe_.wait_ge(identb_ready, 1)
                            pe_.wait_ge(v_evac, 1)
                        pe_.wait_ge(negm_ready, b + 1)
                        wait(pe_, t_evac, t_before_negm(b))
                        pe_.transpose(ps[0:2 * H, 6, 0:P // 2].bitcast(BF16), negm_parts[:, b % 2, :],
                                      identb[:, :]).then_inc(t_ready, 1)
                if step % GROUPS == 2:
                    b = step // GROUPS - 4
                    if 0 <= b < B:
                        pe_.wait_ge(o_done, b + 1)
                        wait(pe_, t_evac, t_before_o(b))
                        pe_.transpose(ps[:, 6, 0:P], o_nat[:, b % 2, :], ident).then_inc(t_ready, 1)
                if step % GROUPS == 3:
                    b = step // GROUPS - 4
                    if 0 <= b < B:
                        pe_.wait_ge(t_evac, t_before_o(b) + 1)
                        if b == 0:
                            pe_.wait_ge(wf_evac, 2)
                        wait(pe_, x1_done, b)
                        pe_.matmul(ps[:, 7, 0:D], o_t[:, b % 2, :], wb[:, W_O:W_O + D], start=True,
                                   stop=True).then_inc(o_proj, 1)
                if step in (STEP_EXP, STEP_EXP + 2):
                    if step == STEP_EXP:
                        pe_.wait_ge(low_done, 1)
                        pe_.wait_ge(wt_evac, 1)
                        pe_.wait_ge(exp_done, NG)
                    up((step - STEP_EXP) // 2)

            def down(u):
                h, e = divmod(u, E)
                y, w = ps[:, 4 + h, :], u % HRING
                cols = slice(2 * D, 3 * D)
                pe_.wait_ge(hi_done, u + 1)
                wait(pe_, w2_lo, min(u, E - 1) + 1)
                pe_.matmul(y, wh[:, e, cols], hh[:, w, :], start=False, stop=False, skip_group_check=True)
                pe_.matmul(y, wl[:, e, cols], hh[:, w, :], start=False, stop=False, skip_group_check=True)
                wait_lo(pe_, u)
                pe_.matmul(y, wh[:, e, cols], hl[:, w, :], start=False, stop=True,
                           skip_group_check=True).then_inc(w2_done, 1)

            def open_sum(h):
                pe_.wait_ge(wt_evac, h + 1)
                pe_.matmul(ps[:, 4 + h, :], b2_twice[:, :], wt_t[:, half(h)], start=True, stop=True).then_inc(b2_mm, 1)

            def y_back(k):
                pe_.wait_ge(y_evac, k + 1)
                for i, b in enumerate(SETS[k]):
                    t = pe_.transpose(ps[:, stage_bank("experts", k), tok(i)], y_t[:, tok(b)], ident)
                t.then_inc(y_tr, 1)

            def queries(k):
                pe_.wait_ge(xn_t_ready, norm_count(3, k))
                pe_.matmul(ps[:, stage_bank("queries", k), set_cols(k)], wb[:, W_Q1:W_Q1 + D], xn_t[:, set_tok(k)],
                           start=True, stop=True).then_inc(q1_mm, 1)

            def scores(k):
                pe_.wait_ge(q1_evac, k + 1)
                for i, b in enumerate(SETS[k]):
                    m = pe_.matmul(ps[:, stage_bank("scores", k), tok(i)], q1_t[:, tok(b)], k1_t[:, tok(b)],
                                   start=True, stop=True)
                m.then_inc(s1_mm, 1)

            def turn_probabilities(k):
                pe_.wait_ge(p_done, k + 1)
                for i, b in enumerate(SETS[k]):
                    t = pe_.transpose(ps[:, stage_bank("probabilities", k), tok(i)], pr[:, b, :], ident)
                t.then_inc(p_tr, 1)

            def by_values(k):
                pe_.wait_ge(p_evac, k + 1)
                for i, b in enumerate(SETS[k]):
                    m = pe_.matmul(ps[:, stage_bank("values", k), tok(i)], pr_t[:, b, :], v1[:, b, :],
                                   start=True, stop=True)
                m.then_inc(av1_mm, 1)

            def last_product(k):
                bank = ps[:, stage_bank("last", k), :]
                pe_.wait_ge(var_ready, norm_count(4, k))
                pe_.matmul(bank[:, set_cols(k)].rearrange("p (b d) -> p b d", d=D), ones_row[:, :],
                           row_sb[0:1, 3 * D:4 * D].unsqueeze(1).broadcast_to([1, len(SETS[k]), D]), start=True,
                           stop=True)
                pe_.wait_ge(xn_t_ready, norm_count(4, k))
                for i, b in enumerate(SETS[k]):
                    m = pe_.matmul(bank[:, tok(i)], xn_t[:, tok(b)], wf[:, 1, :], start=False, stop=True,
                                   skip_group_check=True)
                m.then_inc(f_mm, 1)

            pe_.wait_ge(o_done, B)
            pe_.wait_ge(b2_ready, 1)
            open_sum(0)
            for u in range(STARTED, 2 * E):
                if u == E:
                    pe_.wait_ge(low_done, 2)
                up(u)
                if u >= DOWN_LAG:
                    down(u - DOWN_LAG)
                if u == 4:
                    pe_.wait_ge(x1_done, B)
                    norm_turn(2, 1)
                if u == 6:
                    gate_scores(1)
                if u == 12:
                    turn_weights(1)
                if u == 14:
                    open_sum(1)
                if u == E + 6:
                    y_back(0)
                if u == E + 9:
                    norm_turn(3, 0)
                if u == E + 11:
                    queries(0)
                if u == E + 13:
                    scores(0)
            turn_probabilities(0)
            for u in range(2 * E - DOWN_LAG, 2 * E):
                down(u)
            late = (1, 2)
            for k in late:
                y_back(k)
            by_values(0)
            for k in late:
                norm_turn(3, k)
            for k in late:
                queries(k)
            for k in late:
                scores(k)
            for k in late:
                turn_probabilities(k)
            norm_turn(4, 0)
            for k in late:
                by_values(k)
            last_product(0)
            for k in late:
                norm_turn(4, k)
            for k in late:
                last_product(k)

        @block.vector
        def _(dve):
            chain = [0]

            def link(ins):
                chain[0] += 1
                ins.then_inc(vec, 1)
                dve.wait_ge(vec, chain[0])

            def statistics(src, bs):
                for b in bs:
                    s = dve.bn_stats(stats[:, b, :], src[:, b, :])
                link(s)
                for b in bs:
                    s = dve.bn_aggr(mv[:, b, :], stats[:, b, :])
                link(s)
                dve.tensor_scalar(var_eps[:, bs.start:bs.stop], mv[:, bs.start:bs.stop, 1:2]
                                  .rearrange("p b o -> p (b o)"), EPS, None, ALU.add).then_inc(var_ready, 1)

            def scaled(src, bs):
                for b in bs:
                    s = dve.tensor_scalar(xn[:, b, :], src[:, b, :], mv[:, b, 0:1], rstd[:, b:b + 1], ALU.subtract,
                                          ALU.mult)
                return s

            def normalise(norm, k, src):
                dve.wait_ge(rstd_ready, norm_count(norm, k))
                scaled(src, norm_range(norm, k)).then_inc(xn_ready, 1)

            def norm_low(h):
                dve.wait_ge(xn_t_ready, norm_count(2, h))
                dve.tensor_tensor(xl[:, half(h)], ps[:, norm_bank(2, h), :], xh[:, half(h)].bitcast(F32),
                                  ALU.subtract).then_inc(low_done, 1)

            def gate_out(h):
                dve.wait_ge(gate_mm, h + 1)
                dve.tensor_copy(raw[:, seqs(h), :], ps[:, gate_bank(h), 0:HB * E].rearrange("p (b e) -> p b e", b=HB))\
                    .then_inc(gate_evac, 1)

            def compare_groups(h):
                r, g = raw[:, seqs(h), :], gmax[:, seqs(h), :]
                dve.memset(cand[:, seqs(h), 0:4], BIG)
                dve.wait_ge(gate_evac, h + 1)
                link(dve.tensor_reduce(g.rearrange("p b g -> p (b g)"), r.rearrange("p b (g e) -> p (b g) e", g=G), AX,
                                       ALU.max))
                mine = g.unsqueeze(3).broadcast_to([P, HB, G, G])
                other = g.unsqueeze(2).broadcast_to([P, HB, G, G])
                dve.tensor_tensor(cmp_a[:, seqs(h)], other, mine, ALU.is_gt)
                link(dve.tensor_tensor(cmp_b[:, seqs(h)], other, mine, ALU.is_ge))

            def rank_groups(h):
                above, level, place = cmp_a[:, seqs(h)], cmp_b[:, seqs(h)], rank[:, seqs(h), :]
                before = wb[:, W_LOW:W_LOW + G * G].rearrange("p (g o) -> p g o", g=G).unsqueeze(1)\
                    .broadcast_to([P, HB, G, G])
                link(dve.tensor_tensor(level, level, before, ALU.mult))
                link(dve.tensor_tensor(above, above, level, ALU.max))
                link(dve.tensor_reduce(place, above, AX, ALU.add))

            def candidates(h):
                r, place = raw[:, seqs(h), :], rank[:, seqs(h), :]
                link(dve.tensor_scalar(place, place, 2.0, -BIG, ALU.is_ge, ALU.mult))
                link(dve.tensor_tensor(cand[:, seqs(h), 4:4 + E].rearrange("p b (g e) -> p b g e", g=G),
                                       r.rearrange("p b (g e) -> p b g e", g=G),
                                       place.unsqueeze(3).broadcast_to([P, HB, G, EG]), ALU.add))
                for b in seqs_range(h):
                    m = dve.max(top8[:, b, :], cand[:, b, :])
                link(m)

            def mark_chosen(h):
                for b in seqs_range(h):
                    m = dve.match_replace(left[:, b, :], top8[:, b, :], cand[:, b, :], TAKEN)
                link(m)

            def sigmoids(h):
                sig = sg[:, seqs(h)]
                dve.wait_ge(gate_exp, h + 1)
                link(dve.tensor_scalar(sig, sig, 1.0, None, ALU.add))
                link(dve.reciprocal(sig, sig))

            def share(h):
                sig, chosen, w, total = (t[:, seqs(h)] for t in (sg, left, wts, wsum))
                link(dve.scalar_tensor_tensor(w, chosen[:, :, 4:4 + E], (BIG + TAKEN) / 2, sig, ALU.is_ge, ALU.mult))
                link(dve.tensor_reduce(total, w, AX, ALU.add))
                link(dve.reciprocal(total, total))
                link(dve.tensor_scalar(total, total, ROUTE_SCALE / 2, None, ALU.mult))
                dve.tensor_tensor(w, w, total.unsqueeze(2).broadcast_to([P, HB, E]), ALU.mult).then_inc(wts_ready, 1)

            def weights_out(h):
                dve.wait_ge(wts_tr, h + 1)
                dve.wait_ge(v_done, HALVES)
                dve.tensor_copy(wt_t[:, half(h)], ps[0:E, wts_bank(h), :]).then_inc(wt_evac, 1)

            def low_h(u):
                w = u % HRING
                dve.wait_ge(hi_done, u + 1)
                dve.tensor_tensor(hl[:, w, :], hw[:, w, :], hh[:, w, :].bitcast(F32),
                                  ALU.subtract).then_inc(lo_done[w], 1)

            def product(u):
                e, s = u % E, u % 2
                dve.wait_ge(act_t, u + 1)
                dve.scalar_tensor_tensor(uu[:, s, :], th[:, s, :], 1.0, a1[:, s, :], ALU.add,
                                         ALU.mult).then_inc(vec_u, 1)
                if u + AHEAD < E:
                    split2(u + AHEAD)
                dve.wait_ge(c_ready, u + 1)
                if u >= HRING:
                    dve.wait_ge(hi_done, u - HRING + 1)
                    wait_lo(dve, u - HRING)
                dve.wait_ge(vec_u, u + 1)
                dve.scalar_tensor_tensor(hw[:, u % HRING, :], ps[:, 2 + s, :], bcol[:, e, 2:3], uu[:, s, :], ALU.add,
                                         ALU.mult).then_inc(h0_done, 1)

            def split2(e):
                dve.wait_ge(w_hi, e + 1)
                dve.tensor_tensor(wl[:, e, 2 * D:3 * D], w_of(e)[:, 2 * D:3 * D],
                                  wh[:, e, 2 * D:3 * D].bitcast(F32), ALU.subtract).then_inc(w2_lo, 1)

            for h in range(HALVES):
                dve.wait_ge(x_in[h], 16)
                statistics(x0, seqs_range(h))
            for h in range(HALVES):
                normalise(1, h, x0)
            for n in range(4):
                col = A_COL + (1 - n % 2)
                dve.wait_ge(part1, n + 1)
                wait(dve, part2, n - 1)
                r = rest[:, n % 2, :]
                dve.scalar_tensor_tensor(r, ps[:, n, :], wa[:, col:col + 1], parts[n][:, 0, :], ALU.add,
                                         ALU.subtract).then_inc(rest_ready, 1)
                dve.wait_ge(part2, n + 1)
                dve.tensor_tensor(parts[n][:, 2, :], r, parts[n][:, 1, :], ALU.subtract).then_inc(part3, 1)
            dve.wait_ge(row_in, 16)
            dve.wait_ge(tg_ready, 1)
            dve.scalar_tensor_tensor(x0[:, :, :], row_sb[:, 0:D].unsqueeze(1).broadcast_to([P, B, D]), tg[:, 0:1],
                                     x0[:, :, :], ALU.mult, ALU.add).then_inc(xb_ready, 1)

            for step in range(STEPS):
                j = step
                if j < NG:
                    b, g = divmod(j, GROUPS)
                    dve.wait_ge(s_ready, j + 1)
                    m = dve.tensor_reduce(negm[:, b % 2, g * GH:(g + 1) * GH],
                                          ps[:, j % 2, :].rearrange("p (i k) -> p i k", i=GH), AX, ALU.max,
                                          negate=True)
                    m.then_inc(max_done, 1)
                    if g == GROUPS - 1:
                        dve.wait_ge(max_done, j + 1)
                        wait(dve, t_ready, t_before_negm(b - 2) + 1 if b >= 2 else 0)
                        link(dve.tensor_copy(negm_parts[:, b % 2, 0:H], negm[:, b % 2, :]))
                        dve.tensor_tensor(negm_parts[:, b % 2, H:2 * H], negm[:, b % 2, :], negm_parts[:, b % 2, 0:H],
                                          ALU.subtract).then_inc(negm_ready, 1)
                j = step - ST_LAG - 1
                if 0 <= j < NG and by_vec(j):
                    dve.wait_ge(exp_done, j + 1)
                    wait(dve, av_done, j - RING + 1)
                    dve.tensor_tensor(p2[:, j % RING, :], pe[:, j % RING, :], p1[:, j % RING, :],
                                      ALU.subtract).then_inc(p2_vec, 1)
                if step % GROUPS == 0:
                    b = step // GROUPS - 4
                    if 0 <= b < B:
                        dve.wait_ge(av_done, GROUPS * (b + 1))
                        wait(dve, t_ready, t_before_o(b - 2) + 1 if b >= 2 else 0)
                        o = ps[:, 4 + b % 2, 0:H * VC].rearrange("p (h v) -> p h v", h=H)
                        dve.tensor_reduce(o_sum[:, b % 2, :].rearrange("p (h d) -> p h d", h=H),
                                          o[:, :, 0:3 * HD].rearrange("p h (t d) -> p h d t", t=3), AX, ALU.add)
                        link(dve.reciprocal(den[:, b % 2, :], o[:, :, 3 * HD:VC].rearrange("p h v -> p (h v)")))
                        dve.tensor_tensor(o_nat[:, b % 2, :].rearrange("p (h d) -> p h d", h=H),
                                          o_sum[:, b % 2, :].rearrange("p (h d) -> p h d", h=H),
                                          den[:, b % 2, :].unsqueeze(2).broadcast_to([P, H, HD]),
                                          ALU.mult).then_inc(o_done, 1)
                if step % GROUPS == 0:
                    b = step // GROUPS - 5
                    if 0 <= b < B:
                        dve.wait_ge(o_proj, b + 1)
                        dve.wait_ge(xb_ready, 1)
                        dve.scalar_tensor_tensor(x1[:, b, :], ps[:, 7, 0:D], tg[:, 0:1], x0[:, b, :], ALU.mult,
                                                 ALU.add).then_inc(x1_done, 1)
                if step == STEP_N2:
                    dve.wait_ge(x1_done, HB)
                    statistics(x1, seqs_range(0))
                if step == STEP_N2 + 1:
                    normalise(2, 0, x1)
                if step == STEP_N2 + 5:
                    norm_low(0)
                if step == STEP_N2 + 6:
                    gate_out(0)
                    compare_groups(0)
                    rank_groups(0)
                    candidates(0)
                    mark_chosen(0)
                if step == STEP_N2 + 7:
                    sigmoids(0)
                    share(0)
                if step == STEP_N2 + 9:
                    weights_out(0)
                if step in LOW2_STEPS:
                    split2(LOW2_STEPS.index(step))
                if step in (STEP_EXP + 1, STEP_EXP + 3):
                    product((step - STEP_EXP - 1) // 2)

            def after_experts(k):
                dve.wait_ge(y_tr, k + 1)
                link(dve.scalar_tensor_tensor(flat(x2[:, set_seqs(k), :]), ps[:, stage_bank("experts", k), set_cols(k)],
                                              tg[:, 2:3], flat(x1[:, set_seqs(k), :]), ALU.mult, ALU.add))
                statistics(x2, SETS[k])

            def maxima(k):
                dve.wait_ge(s1_mm, k + 1)
                link(dve.tensor_reduce(negm1[:, 0, set_seqs(k)],
                                       ps[:, stage_bank("scores", k), set_cols(k)].rearrange("p (b k) -> p b k", k=P),
                                       AX, ALU.max, negate=True))
                dve.tensor_scalar(negm1[:, 1, set_seqs(k)], negm1[:, 0, set_seqs(k)], scale1, None,
                                  ALU.mult).then_inc(negm1_done, 1)

            def probabilities_out(k):
                dve.wait_ge(p_tr, k + 1)
                dve.tensor_copy(flat(pr_t[:, set_seqs(k), :]),
                                ps[:, stage_bank("probabilities", k), set_cols(k)]).then_inc(p_evac, 1)
                link(dve.reciprocal(den1[:, 1, set_seqs(k)], den1[:, 0, set_seqs(k)]))
                link(dve.tensor_scalar(den1[:, 1, set_seqs(k)], den1[:, 1, set_seqs(k)], tg[:, 1:2], None, ALU.mult))

            def after_attention(k):
                dve.wait_ge(av1_mm, k + 1)
                for i, b in enumerate(SETS[k]):
                    m = dve.scalar_tensor_tensor(x3[:, b, :], ps[:, stage_bank("values", k), tok(i)],
                                                 den1[:, 1, b:b + 1], x2[:, b, :], ALU.mult, ALU.add)
                link(m)
                statistics(x3, SETS[k])

            def result(k):
                dve.wait_ge(f_tanh, k + 1)
                dve.scalar_tensor_tensor(x4[:, set_seqs(k), :], fft[:, set_seqs(k), :], tg[:, 3:4],
                                         x3[:, set_seqs(k), :], ALU.mult, ALU.add).then_inc(x4_done, 1)

            dve.wait_ge(x1_done, B)
            statistics(x1, seqs_range(1))
            for u in range(STARTED, 2 * E):
                if u >= 3 and not low_by_pool(u - 3):
                    low_h(u - 3)
                product(u)
                if u == 2:
                    normalise(2, 1, x1)
                if u == 5:
                    norm_low(1)
                if u == 6:
                    gate_out(1)
                    compare_groups(1)
                if u == 7:
                    rank_groups(1)
                if u == 8:
                    candidates(1)
                if u == 9:
                    mark_chosen(1)
                    sigmoids(1)
                if u == 10:
                    share(1)
                if u == 13:
                    weights_out(1)
                if u == E + 6:
                    after_experts(0)
                if u == E + 8:
                    normalise(3, 0, x2)
                if u == E + 13:
                    maxima(0)
            for u in range(2 * E - 3, 2 * E):
                low_h(u)
            probabilities_out(0)
            late = (1, 2)
            for k in late:
                after_experts(k)
            for k in late:
                normalise(3, k, x2)
            after_attention(0)
            for k in late:
                maxima(k)
            normalise(4, 0, x3)
            for k in late:
                probabilities_out(k)
            for k in late:
                after_attention(k)
            for k in late:
                normalise(4, k, x3)
            result(0)
            for k in late:
                result(k)


def kernel(**inputs):
    import concourse.bacc as bacc
    from concourse.bass_utils import run_bass_kernel_spmd

    v = {name: np.asarray(a) for name, a in inputs.items()}

    def by_depth(a):
        return a.reshape(H, HD, -1).transpose(1, 0, 2).reshape(D, -1)

    low = np.tril(np.ones((G, G), np.float32), -1).reshape(1, G * G)
    arrays = {
        "x": v["x"],
        "ctx_t": v["ctx_1024"].reshape(T, D).T,
        "w_a": np.concatenate([
            by_depth(v["L0_xattn_wk"]).T, by_depth(v["L0_xattn_wq"]).T, np.eye(P, dtype=np.float32),
            by_depth(v["L0_xattn_bq"]), by_depth(v["L0_xattn_bk"]),
            v["L1_xattn_bq"][:, None], v["L1_xattn_bk"][:, None]], axis=1),
        "w_b": np.concatenate([
            v["L0_xattn_wv"].T, v["L1_xattn_Wv"], v["L0_xattn_wo"].T, v["L1_xattn_Wq"], v["L1_xattn_Wk"],
            v["L1_ffn_weight"].T, v["L1_ffn_aux_weight1"].T, v["L1_ffn_aux_weight2"], v["L0_ffn_Wg"].T,
            np.repeat(low, P, axis=0)], axis=1),
        "rows": np.concatenate([v["L0_xattn_bo"], v["L0_xattn_bv"], v["L1_xattn_bv"], v["L1_ffn_bias"]])[None],
        "gates": np.concatenate([v["g_xattn"], v["g_ffn"]])[None],
        "b2": v["L0_ffn_b2"],
        "w_big": np.concatenate([v[n].transpose(2, 0, 1) for n in ("L0_ffn_W1", "L0_ffn_W3", "L0_ffn_W2")], axis=2),
        "b_cols": np.stack([v["L0_ffn_b1"].T, v["L0_ffn_b3"].T], axis=2),
    }
    nc = bacc.Bacc("TRN2", target_bir_lowering=False, num_devices=1)
    args = []
    for name in arrays:
        arrays[name] = np.ascontiguousarray(arrays[name])
        args.append(nc.dram_tensor(name, arrays[name].shape, F32, kind="ExternalInput").ap())
    args.append(nc.dram_tensor("out", (B, P, D), F32, kind="ExternalOutput").ap())
    flamingo(nc, *args)
    done = run_bass_kernel_spmd(nc, [arrays], core_ids=[0])
    return done.results[0]["out"]
```
